# Optimizing a Trainium2 kernel written in Bass

```python
import numpy as np
import jax
import jax.numpy as jnp

def _softmax(x, axis=-1):
    return jax.nn.softmax(x, axis=axis)

def _gelu(x):
    return jax.nn.gelu(x, approximate=True)

def _silu(x):
    return jax.nn.silu(x)

def _sigmoid(x):
    return jax.nn.sigmoid(x)

def _layernorm(x, axis=-1, eps=1e-05):
    m = jnp.mean(x, axis=axis, keepdims=True)
    v = jnp.var(x, axis=axis, keepdims=True)
    return (x - m) / jnp.sqrt(v + eps)

def _scatter_add(tgt, idx, src, axis=0):
    return tgt.at[idx].add(src)

def _segment_sum(src, seg, n):
    return jax.ops.segment_sum(src, seg, n)
kernel_name = 'mk_seq_preln_d1_jaxref_r8_c20f1e'

def setup_inputs(seed: int=0):
    np.random.seed(seed)
    _w = jnp.asarray

    def _L0_attn_setup():
        import jax, jax.numpy as jnp
        import numpy as np
        DIM_IN, DIM_OUT, DIM_INNER = (128, 128, 64)
        key = jax.random.key(seed)
        k1, k2, k3, k4 = jax.random.split(key, 4)
        x = jax.random.normal(k1, (4, 256, DIM_IN), dtype=jnp.float32)
        w_qkv = jax.random.uniform(k2, (DIM_INNER * 3, DIM_IN), dtype=jnp.float32, minval=-1.0, maxval=1.0) / np.sqrt(DIM_IN)
        w_out = jax.random.uniform(k3, (DIM_OUT, DIM_INNER), dtype=jnp.float32, minval=-1.0, maxval=1.0) / np.sqrt(DIM_INNER)
        b_out = jax.random.uniform(k4, (DIM_OUT,), dtype=jnp.float32, minval=-1.0, maxval=1.0) / np.sqrt(DIM_INNER)
        return {'x': x, 'w_qkv': w_qkv, 'w_out': w_out, 'b_out': b_out}
    _L0_attn_in = _L0_attn_setup()

    def _L0_ffn_setup():
        import jax, jax.numpy as jnp
        import numpy as np
        B, S, D, E, F, TOP_K = (4, 256, 128, 8, 512, 2)
        key = jax.random.key(seed)
        k0, k1, k2, k3 = jax.random.split(key, 4)
        init = lambda k, shape, fan: (jax.random.normal(k, shape, jnp.float32) / np.sqrt(fan)).astype(jnp.float32)
        return {'x': jax.random.normal(k0, (B, S, D), jnp.float32), 'gate_w': init(k1, (D, E), D), 'w1': init(k2, (E, D, F), D), 'b1': jnp.zeros((E, F), jnp.float32), 'w2': init(k3, (E, F, D), F), 'b2': jnp.zeros((E, D), jnp.float32)}
    _L0_ffn_in = _L0_ffn_setup()
    _d = {'L0_attn_x': _L0_attn_in['x'], 'L0_attn_w_qkv': _L0_attn_in['w_qkv'], 'L0_attn_w_out': _L0_attn_in['w_out'], 'L0_attn_b_out': _L0_attn_in['b_out'], 'L0_ffn_gate_w': _L0_ffn_in['gate_w'], 'L0_ffn_w1': _L0_ffn_in['w1'], 'L0_ffn_b1': _L0_ffn_in['b1'], 'L0_ffn_w2': _L0_ffn_in['w2'], 'L0_ffn_b2': _L0_ffn_in['b2']}
    _x0 = _d['L0_attn_x']
    _d['L0_attn_x'] = jax.random.normal(jax.random.fold_in(jax.random.key(seed), 1), (2, 2048, 128), dtype=_x0.dtype)
    del _x0
    return _d

def reference(L0_attn_x, L0_attn_w_qkv, L0_attn_w_out, L0_attn_b_out, L0_ffn_gate_w, L0_ffn_w1, L0_ffn_b1, L0_ffn_w2, L0_ffn_b2):

    def _L0_attn_ref(x, w_qkv, w_out, b_out):
        import jax, jax.numpy as jnp
        import numpy as np
        DIM_IN, DIM_OUT, DIM_INNER = (128, 128, 64)
        scale = DIM_INNER ** (-0.5)
        qkv = jnp.einsum('bnd,ed->bne', x, w_qkv)
        q, k, v = jnp.split(qkv, 3, axis=-1)
        sim = jnp.einsum('bid,bjd->bij', q, k) * scale
        n = sim.shape[-1]
        causal = jnp.tril(jnp.ones((n, n), dtype=bool))
        sim = jnp.where(causal[None], sim, -jnp.finfo(sim.dtype).max)
        attn = jax.nn.softmax(sim, axis=-1)
        out = jnp.einsum('bij,bjd->bid', attn, v)
        return jnp.einsum('bnd,od->bno', out, w_out) + b_out

    def _L0_ffn_ref(x, gate_w, w1, b1, w2, b2):
        import jax, jax.numpy as jnp
        import numpy as np
        B, S, D, E, F, TOP_K = (4, 256, 128, 8, 512, 2)
        b, s, d = x.shape
        e = gate_w.shape[1]
        xf = x.reshape(-1, d)
        t = xf.shape[0]
        logits = xf @ gate_w
        top_w, top_idx = jax.lax.top_k(logits, TOP_K)
        top_w = jax.nn.softmax(top_w.astype(jnp.float32), axis=-1).astype(x.dtype)
        combine = jnp.zeros((t, e), x.dtype).at[jnp.arange(t)[:, None], top_idx].add(top_w)
        h = jax.nn.gelu(jnp.einsum('td,edf->tef', xf, w1) + b1, approximate=False)
        y = jnp.einsum('tef,efd->ted', h, w2) + b2
        out = jnp.einsum('ted,te->td', y, combine)
        return out.reshape(b, s, d)
    x = L0_attn_x
    x = x + _L0_attn_ref(_layernorm(x, axis=-1), L0_attn_w_qkv, L0_attn_w_out, L0_attn_b_out)
    x = x + _L0_ffn_ref(_layernorm(x, axis=-1), L0_ffn_gate_w, L0_ffn_w1, L0_ffn_b1, L0_ffn_w2, L0_ffn_b2)
    return x

_drawn_inputs = setup_inputs


def setup_inputs(seed=0):
    import zlib

    import numpy as np

    out = dict(_drawn_inputs(seed))
    spreads = {'L0_ffn_b1': (0.0, 0.1), 'L0_ffn_b2': (0.0, 0.1)}
    factors = {}
    for name, (base, spread) in spreads.items():
        noise = np.random.default_rng([zlib.crc32(name.encode()), seed]).standard_normal(out[name].shape)
        drawn = base * np.exp(spread * noise) if base else spread * noise
        out[name] = jnp.asarray(drawn.astype(out[name].dtype))
    for name, factor in factors.items():
        out[name] = (out[name] * factor).astype(out[name].dtype)
    return out
```

```python
import concourse.bass as bass
from concourse import mybir
from contextlib import ExitStack


def preln_attention_moe(nc, x, w_qkv, w_out, b_out, gate_w, w1, b1, w2, b2, out):
    f32, f32r, bf16 = mybir.dt.float32, mybir.dt.float32r, mybir.dt.bfloat16
    i32, u32 = mybir.dt.int32, mybir.dt.uint32
    ALU, ACT, AX = mybir.AluOpType, mybir.ActivationFunctionType, mybir.AxisListType

    P = 128
    B, S, D = x.shape
    DH = w_out.shape[1]
    E, _, F = w1.shape
    TOP = 2
    T = B * S
    NT = T // P
    GT = 4
    GQ = GT * P
    NG = NT // GT
    GB = S // GQ
    FC = F // P
    SCALE = float(DH) ** -0.5
    EPS = 1e-5
    NEG = -1e38
    REGION = T + P
    ROW = D + 2
    NSLOT = T * TOP
    MAXT = NSLOT // P + E - 1
    UN = 4
    NTILE = -(-MAXT // UN) * UN
    FAR = 1 << 20

    N_FILLS, N_CONSTS = 20, 9

    xf = x.rearrange("b n d -> (b n) d")
    of = out.rearrange("b n d -> (b n) d")
    disp = nc.dram_tensor("dispatched_rows", (E * REGION + P, ROW), f32, kind="Internal").ap()
    ys = nc.dram_tensor("expert_results", (NSLOT, D), f32, kind="Internal").ap()

    def steps(g):
        pairs = [[(kb, 0, GQ, 0), (kb + 1, 0, GQ, GQ)] for kb in range(0, GT * g, 2)]
        k0 = GT * g
        pairs.append([(k0, 0, GQ, 0), (k0 + 1, P, GQ - P, GQ)])
        pairs.append([(k0 + 2, 2 * P, GQ - 2 * P, 0), (k0 + 3, 3 * P, GQ - 3 * P, GQ - 2 * P)])
        return pairs

    def front(G):
        g = G % GB
        return ([("LN1", G, 0), ("XT", G, 0), ("QP", G, 0), ("KP", G, 0), ("VP", G, 0)]
                + [("MX", G, (t, c)) for t in range(GT) for c in range(g + 1)] + [("MR", G, 0)])

    def back(G):
        return [("OE", G, 0), ("OP", G, 0), ("OP", G, 1), ("LN2", G, 0), ("X2T", G, 0),
                ("LG", G, 0), ("RT", G, 0), ("RK", G, 0), ("SC", G, 0)]

    def spread(main, side):
        res, k = [], 0
        for i, m in enumerate(main):
            res.append(m)
            n = (i + 1) * len(side) // len(main)
            res += side[k:n]
            k = n
        return res

    SCHEDULE = front(0)
    for G in range(NG):
        side = (back(G - 1) if G else []) + (front(G + 1) if G + 1 < NG else [])
        SCHEDULE += spread([("AS", G, j) for j in range(len(steps(G % GB)))], side)
    SCHEDULE += [("AE", NG - 1, 0)] + back(NG - 1) + [("CN", NG - 1, 0)]

    FIRST_STEP = [0]
    for G in range(NG):
        FIRST_STEP.append(FIRST_STEP[-1] + len(steps(G % GB)))

    READERS = {"XT": "a", "QP": "av", "KP": "av", "VP": "a", "MX": "v", "MR": "a",
               "OP": "v", "X2T": "a", "LG": "v", "RK": "v", "CN": "v"}
    ITEM, ACT_READS, DVE_READS = {}, [], []
    for part in SCHEDULE:
        if part[0] in READERS:
            who = READERS[part[0]]
            ITEM[part] = len(ITEM)
            ACT_READS.append((ACT_READS[-1] if ACT_READS else 0) + ("a" in who))
            DVE_READS.append((DVE_READS[-1] if DVE_READS else 0) + ("v" in who))

    ctx = ExitStack()
    with ctx:
        def sb(name, shape, dt=f32):
            return ctx.enter_context(nc.sbuf_tensor(name, shape, dt))

        def pb(name, shape, dt=f32):
            return ctx.enter_context(nc.psum_tensor(name, shape, dt))

        def sem(name):
            return ctx.enter_context(nc.semaphore(name))

        ident = sb("ident", [P, P])
        ident_r = sb("ident_r", [P, P], f32r)
        ident_b = sb("ident_b", [P, P], bf16)
        mask_kq = sb("mask_kq", [P, P], bf16)
        mask_qk = sb("mask_qk", [P, P], bf16)
        tri = sb("tri", [P, P], bf16)
        ones_b = sb("ones_b", [P, P], bf16)
        ones_r = sb("ones_r", [2, P], f32r)
        mhalf = sb("mhalf", [P, GT])
        expert_id = sb("expert_id", [P, E])
        dest = sb("dest", [P, NT, TOP], i32)
        tile_no_i = sb("tile_no_i", [P, NTILE], i32)
        expert_i = sb("expert_i", [P, E], i32)
        tile_no = sb("tile_no", [P, NTILE])
        incl = sb("incl", [P, E, E])
        wq2, wk2, wv_ = sb("wq2", [P, D]), sb("wk2", [P, D]), sb("wv_", [DH, D])
        wo2 = sb("wo2", [P, 2 * DH])
        wqT, wkT, wvT = sb("wqT", [D, P]), sb("wkT", [D, P]), sb("wvT", [D, DH])
        wo_aug = sb("wo_aug", [DH + 1, D + 1])
        gate = sb("gate", [D, E])
        w1_sb = sb("w1_sb", [P, E * F])
        w2_sb = sb("w2_sb", [P, E * FC * D])
        NB1, NB2 = E * F // P, E * D // P
        b_raw = sb("b_raw", [P, NB1 + NB2])
        b_hi = sb("b_hi", [P, NB1 + NB2], f32r)
        b_lo = sb("b_lo", [P, NB1 + NB2], f32r)
        b1_r = sb("b1_r", [2, E * F], f32r)
        b2_r = sb("b2_r", [2, E * D], f32r)
        xs_ = sb("xs_", [P, NT, D])
        stats = sb("stats", [P, GT, 6])
        mv = sb("mv", [P, GT, 2])
        veps = sb("veps", [P, GT])
        rstd = sb("rstd", [P, GT])
        mv2 = sb("mv2", [P, GT, 2])
        veps2 = sb("veps2", [P, GT])
        rstd2 = sb("rstd2", [P, GT])
        xn = sb("xn", [P, 2, GT, D])
        xT = sb("xT", [D, 2, GQ])
        q_hi = sb("q_hi", [P, 2, GQ], f32r)
        q_lo = sb("q_lo", [DH + 1, 2, GQ], f32r)
        k_hl = sb("k_hl", [P, T], f32r)
        k_h1 = sb("k_h1", [DH + 1, T], f32r)
        V = sb("V", [P, NT, DH + 1])
        mpart = sb("mpart", [P, GT, GB])
        mneg = sb("mneg", [P, GT, DH + 2], f32r)
        prob = sb("prob", [P, 2, 2 * GQ])
        oT = sb("oT", [DH + 1, 2, GQ])
        rsum = sb("rsum", [P, 2])
        rows = sb("rows", [P, 2, GT, TOP, ROW])
        x2T = sb("x2T", [D, GQ])
        lg = sb("lg", [P, GT, E])
        top8 = sb("top8", [P, GT, 8])
        top_i = sb("top_i", [P, GT, 8], u32)
        top_f = sb("top_f", [P, GT, TOP])
        pick = sb("pick", [P, TOP, GT, E])
        both = sb("both", [P, GT, E], bf16)
        bothsum = sb("bothsum", [P, E])
        seen = sb("seen", [P, E])
        seen_b = sb("seen_b", [P, E], bf16)
        gap = sb("gap", [P, GT])
        egap = sb("egap", [P, GT])
        rank = sb("rank", [P, GT, E])
        ranked = sb("ranked", [P, TOP, GT, E])
        slot_f = sb("slot_f", [P, TOP, GT])
        slot = sb("slot", [P, 2, TOP, GT], u32)
        cnt = sb("cnt", [P, E])
        cnt_i = sb("cnt_i", [P, E], i32)
        pad_at = sb("pad_at", [P, E], i32)
        nt_i = sb("nt_i", [P, E], i32)
        nt_f = sb("nt_f", [P, E])
        cum8 = sb("cum8", [P, E, E])
        cend = sb("cend", [P, E])
        skip = sb("skip", [P, E])
        past = sb("past", [P, NTILE, E])
        past2 = sb("past2", [P, NTILE, E])
        te_f = sb("te_f", [P, NTILE])
        tr_f = sb("tr_f", [P, NTILE])
        tile_expert = sb("tile_expert", [P, NTILE], i32)
        tile_row = sb("tile_row", [P, NTILE], i32)
        pad_rows = sb("pad_rows", [P, ROW])
        xg = sb("xg", [P, UN, ROW])
        xgT = sb("xgT", [D, 2, P])
        h = sb("h", [P, 2, F])
        hT = sb("hT", [P, 2, F])
        y = sb("y", [P, UN, D])
        yg = sb("yg", [P, 2, GT, TOP * D])

        st = [pb(f"st{i}", [P, 2 * GQ]) for i in range(2)]
        pv = [pb(f"pv{i}", [P, GQ]) for i in range(2)]
        wk = [pb(f"wk{i}", [P, GQ]) for i in range(2)]

        x_in = [sem(f"x_in{G}") for G in range(NG)]
        wqkv_in, wout_in, gate_in, w12_in = sem("wqkv_in"), sem("wout_in"), sem("gate_in"), sem("w12_in")
        b_in, bias_split, bias_in = sem("b_in"), sem("bias_split"), sem("bias_in")
        consts0, consts = sem("consts0"), sem("consts")
        wT_ready, wT_copied = sem("wT_ready"), sem("wT_copied")
        vec = sem("vec")
        var_ready, rstd_ready = sem("var_ready"), sem("rstd_ready")
        xn_ready, xT_ready = sem("xn_ready"), sem("xT_ready")
        q_hi_ready, q_lo_ready = sem("q_hi_ready"), sem("q_lo_ready")
        k_hi_ready, k_lo_ready, k_h1_ready, v_ready = (sem("k_hi_ready"), sem("k_lo_ready"),
                                                       sem("k_h1_ready"), sem("v_ready"))
        mneg_ready, mrow_ready = sem("mneg_ready"), sem("mrow_ready")
        bank_full, bank_act, bank_dve = sem("bank_full"), sem("bank_act"), sem("bank_dve")
        scores_ready, probs_ready, pv_done = sem("scores_ready"), sem("probs_ready"), sem("pv_done")
        oT_ready, x2_ready = sem("oT_ready"), sem("x2_ready")
        var2_ready, rstd2_ready = sem("var2_ready"), sem("rstd2_ready")
        x2n_ready, x2T_ready = sem("x2n_ready"), sem("x2T_ready")
        gap_ready, egap_ready, picks_ready = sem("gap_ready"), sem("egap_ready"), sem("picks_ready")
        slots_ready = sem("slots_ready")
        sent = [sem(f"sent{i}") for i in range(2)]
        counts_ready, pad_at_ready, table_ready, padded = (sem("counts_ready"), sem("pad_at_ready"),
                                                           sem("table_ready"), sem("padded"))
        xg_in = [sem(f"xg_in{u}") for u in range(UN)]
        xgT_full, xgT_ready = sem("xgT_full"), sem("xgT_ready")
        h_full, h_ready = sem("h_full"), sem("h_ready")
        hT_full, hT_ready = sem("hT_full"), sem("hT_ready")
        y_full, y_ready = sem("y_full"), sem("y_ready")
        scatters_begun = sem("scatters_begun")
        y_sent = [sem(f"y_sent{u}") for u in range(UN)]
        yg_in = [sem(f"yg_in{i}") for i in range(2)]
        out_ready, stored = sem("out_ready"), sem("stored")

        block = ctx.enter_context(nc.Block())

        def item(stage, G, n=0):
            return ITEM[(stage, G, n)] + 1

        def bank(stage, G, n=0):
            return wk[ITEM[(stage, G, n)] % 2]

        def wait_count(eng, semaphore, n):
            if not (isinstance(n, int) and n <= 0):
                eng.wait_ge(semaphore, n)

        def expert_rounds(eng, step):
            for u in range(UN):
                step(0, u, lambda k: u + k >= 0)
            with eng.Fori(1, NTILE // UN - 1) as turn:
                for u in range(UN):
                    step(turn * UN, u, lambda k: True)
            for u in range(UN):
                step(NTILE - UN, u, lambda k: u + k < UN)

        def yload(G):
            return ys[G * GQ * TOP:(G + 1) * GQ * TOP, :].rearrange("(t p k) d -> p t (k d)", p=P, k=TOP)

        @block.sync
        def _(sp):
            for G in range(NG):
                sp.dma_start(xs_[:, G * GT:(G + 1) * GT, :],
                             xf[G * GQ:(G + 1) * GQ, :].rearrange("(t p) d -> p t d", p=P)).then_inc(x_in[G], 16)
                if G == 0:
                    for i in range(2):
                        sp.dma_start(wq2[i * DH:(i + 1) * DH, :], w_qkv[0:DH, :]).then_inc(wqkv_in, 16)
                        sp.dma_start(wk2[i * DH:(i + 1) * DH, :], w_qkv[DH:2 * DH, :]).then_inc(wqkv_in, 16)
                    sp.dma_start(wv_[:, :], w_qkv[2 * DH:3 * DH, :]).then_inc(wqkv_in, 16)
                    sp.dma_start(wo2[:, 0:DH], w_out).then_inc(wqkv_in, 16)
                    sp.dma_start(wo2[:, DH:], w_out).then_inc(wqkv_in, 16)
                    sp.dma_start(wo_aug[DH:DH + 1, 0:D], b_out.rearrange("(a n) -> a n", a=1)).then_inc(wout_in, 16)
                    sp.dma_start(gate[:, :], gate_w).then_inc(gate_in, 16)
                    sp.dma_start(b_raw[:, 0:NB1], b1.rearrange("e f -> (e f)").rearrange("(p n) -> p n", p=P)).then_inc(b_in, 16)
                    sp.dma_start(b_raw[:, NB1:], b2.rearrange("e d -> (e d)").rearrange("(p n) -> p n", p=P)).then_inc(b_in, 16)
            sp.dma_start(w1_sb[:, :].rearrange("p (e f) -> p e f", e=E), w1.rearrange("e d f -> d e f")).then_inc(w12_in, 16)
            sp.dma_start(w2_sb[:, :].rearrange("p (e c d) -> p e c d", e=E, c=FC),
                         w2.rearrange("e (c p) d -> p e c d", p=P)).then_inc(w12_in, 16)
            sp.wait_ge(bias_split, 2)
            for i, part in enumerate((b_hi, b_lo)):
                sp.dma_start(b1_r[i:i + 1, :].bitcast(f32), part[:, 0:NB1].bitcast(f32)).then_inc(bias_in, 16)
                sp.dma_start(b2_r[i:i + 1, :].bitcast(f32), part[:, NB1:].bitcast(f32)).then_inc(bias_in, 16)
            sp.wait_ge(consts0, N_FILLS)
            sp.dma_start(disp[E * REGION:E * REGION + P, :], pad_rows[:, :]).then_inc(padded, 16)
            sp.wait_ge(pad_at_ready, 1)
            for e in range(E):
                at = sp.value_load(pad_at[0:1, e:e + 1], min_val=e * REGION, max_val=e * REGION + T)
                sp.dma_start(disp[bass.ds(at, P), :], pad_rows[:, :]).then_inc(padded, 16)
            for i in range(2):
                sp.wait_ge(sent[i], 16 * TOP * GT * (NG // 2))
            sp.wait_ge(padded, 16 * (E + 1))
            sp.wait_ge(table_ready, 1)

            def load_rows(base, u):
                at = sp.value_load(tile_row[0:1, bass.ds(base + u, 1)], min_val=0, max_val=E * REGION)
                wait_count(sp, y_sent[u], 4 * base)
                sp.dma_start(xg[:, u, :], disp[bass.ds(at, P), :]).then_inc(xg_in[u], 16)

            for u in range(UN):
                load_rows(0, u)
            with sp.Fori(1, NTILE // UN) as turn:
                for u in range(UN):
                    load_rows(turn * UN, u)

            for u in range(UN):
                sp.wait_ge(y_sent[u], 16 * (NTILE // UN))
            for G in range(NG):
                if G >= 2:
                    sp.wait_ge(out_ready, G - 1)
                sp.dma_start(yg[:, G % 2], yload(G)).then_inc(yg_in[G % 2], 16)

        @block.gpsimd
        def _(pool):
            g = nc.gpsimd
            g.memset(wo_aug[0:DH, D:D + 1], 0.0).then_inc(consts0, 1)
            g.memset(ident[:, :], 0.0).then_inc(consts0, 1)
            g.memset(mask_kq[:, :], 0.0).then_inc(consts0, 1)
            g.memset(mask_qk[:, :], 0.0).then_inc(consts0, 1)
            g.memset(tri[:, :], 1.0).then_inc(consts0, 1)
            g.memset(incl[:, :, :], 1.0).then_inc(consts0, 1)
            g.memset(ones_b[:, :], 1.0).then_inc(consts0, 1)
            g.memset(ones_r[:, :].bitcast(f32), 1.0).then_inc(consts0, 1)
            g.memset(mhalf[:, :], -0.5).then_inc(consts0, 1)
            g.memset(mneg[:, :, :].bitcast(f32), 0.0).then_inc(consts0, 1)
            g.memset(V[:, :, DH:DH + 1], 1.0).then_inc(consts0, 1)
            g.memset(seen[:, :], 0.0).then_inc(consts0, 1)
            g.memset(seen_b[:, :], 0.0).then_inc(consts0, 1)
            g.memset(pad_rows[:, 0:D + 1], 0.0).then_inc(consts0, 1)
            g.memset(pad_rows[:, D + 1:ROW].bitcast(i32), FAR).then_inc(consts0, 1)
            g.iota(tile_no_i[:, :], [[1, NTILE]], base=0, channel_multiplier=0).then_inc(consts0, 1)
            g.iota(expert_i[:, :], [[1, E]], base=0, channel_multiplier=0).then_inc(consts0, 1)
            g.iota(dest[:, :, :], [[TOP * P, NT], [1, TOP]], base=0, channel_multiplier=TOP).then_inc(consts0, 1)
            pool.wait_ge(consts0, N_FILLS)
            g.affine_select(out=ident[:, :], in_=ident[:, :], compare_op=ALU.not_equal, fill=1.0, base=0,
                            pattern=[[-1, P]], channel_multiplier=1).then_inc(consts, 1)
            g.affine_select(out=mask_kq[:, :], in_=mask_kq[:, :], compare_op=ALU.is_ge, fill=NEG, base=0,
                            pattern=[[1, P]], channel_multiplier=-1).then_inc(consts, 1)
            g.affine_select(out=mask_qk[:, :], in_=mask_qk[:, :], compare_op=ALU.is_ge, fill=NEG, base=0,
                            pattern=[[-1, P]], channel_multiplier=1).then_inc(consts, 1)
            g.affine_select(out=tri[:, :], in_=tri[:, :], compare_op=ALU.is_gt, fill=0.0, base=0,
                            pattern=[[1, P]], channel_multiplier=-1).then_inc(consts, 1)
            g.affine_select(out=incl[:, :, :], in_=incl[:, :, :], compare_op=ALU.is_ge, fill=0.0, base=0,
                            pattern=[[1, E], [-1, E]], channel_multiplier=0).then_inc(consts, 1)
            g.tensor_copy(tile_no[:, :], tile_no_i[:, :]).then_inc(consts, 1)
            g.tensor_copy(expert_id[:, :], expert_i[:, :]).then_inc(consts, 1)
            pool.wait_ge(consts, 1)
            g.tensor_copy(ident_r[:, :], ident[:, :]).then_inc(consts, 1)
            g.tensor_copy(ident_b[:, :], ident[:, :]).then_inc(consts, 1)

            for stage, G, n in SCHEDULE:
                r = G % 2
                if stage == "LN1":
                    pool.wait_ge(var_ready, G + 1)
                    wait_count(pool, xn_ready, G)
                    g.tensor_tensor(rstd[:, :], veps[:, :], mhalf[:, :], ALU.pow).then_inc(rstd_ready, 1)
                elif stage == "LN2":
                    pool.wait_ge(var2_ready, G + 1)
                    wait_count(pool, x2n_ready, G)
                    g.tensor_tensor(rstd2[:, :], veps2[:, :], mhalf[:, :], ALU.pow).then_inc(rstd2_ready, 1)
                elif stage == "SC":
                    pool.wait_ge(slots_ready, G + 1)
                    for t in range(GT):
                        for k in range(TOP):
                            g.indirect_dma_start(
                                out=disp, out_offset=bass.IndirectOffsetOnAxis(ap=slot[:, r, k, t:t + 1], axis=0),
                                in_=rows[:, r, t, k, :], in_offset=None).then_inc(sent[r], 16)

            bound = pool.to_reg(NSLOT - 1)

            def step(base, u, has):
                pool.wait_ge(y_ready, base + u + 1)
                pool.sem_inc(scatters_begun, 1)
                g.indirect_dma_start(
                    out=ys, out_offset=bass.IndirectOffsetOnAxis(ap=xg[:, u, D + 1:ROW].bitcast(u32), axis=0),
                    in_=y[:, u, :], in_offset=None, bounds_check=bound, oob_is_err=False).then_inc(y_sent[u], 16)

            expert_rounds(pool, step)

        @block.scalar
        def _(act):
            a = nc.scalar
            copy = ACT.Copy
            act.wait_ge(wT_ready, 1)
            a.activation(wqT[:, :], st[0][:, 0:P], copy).then_inc(wT_copied, 1)
            a.activation(wkT[:, :], st[0][:, P:2 * P], copy).then_inc(wT_copied, 1)
            a.activation(wvT[:, :], st[0][:, 2 * P:2 * P + DH], copy).then_inc(wT_copied, 1)
            a.activation(wo_aug[0:DH, 0:D], st[0][0:DH, 3 * P:4 * P], copy).then_inc(wT_copied, 1)

            for stage, G, n in SCHEDULE:
                r, cols = G % 2, slice(G * GQ, (G + 1) * GQ)
                if stage in READERS and "a" in READERS[stage]:
                    act.wait_ge(bank_full, item(stage, G, n))
                    ps = bank(stage, G, n)
                if stage == "XT":
                    if G >= 2:
                        act.wait_ge(bank_full, item("VP", G - 2))
                    a.activation(xT[:, r], ps[:, :], copy).then_inc(bank_act, 1)
                elif stage == "QP":
                    if G >= 2:
                        act.wait_ge(scores_ready, FIRST_STEP[G - 1])
                    a.activation(q_hi[:, r], ps[:, :], copy).then_inc(bank_act, 1)
                elif stage == "KP":
                    a.activation(k_hl[:, cols], ps[:, :], copy).then_inc(k_hi_ready, 1)
                    a.activation(k_h1[0:DH, cols], ps[0:DH, :], copy).then_inc(bank_act, 1)
                elif stage == "VP":
                    a.activation(V[:, G * GT:(G + 1) * GT, 0:DH],
                                 ps[:, 0:GT * DH].rearrange("p (t d) -> p t d", t=GT), copy).then_inc(bank_act, 1)
                elif stage == "MR":
                    if G >= 2:
                        act.wait_ge(scores_ready, FIRST_STEP[G - 1])
                    a.activation(q_lo[DH:DH + 1, r, :], ps[DH:DH + 1, :], copy).then_inc(bank_act, 1)
                elif stage == "AS":
                    s = FIRST_STEP[G] + n
                    act.wait_ge(scores_ready, s + 1)
                    wait_count(act, pv_done, s - 1)
                    width = sum(w for _, _, w, _ in steps(G % GB)[n])
                    a.activation(prob[:, s % 2, 0:width], st[s % 2][:, 0:width], ACT.Exp,
                                 scale=SCALE).then_inc(probs_ready, 1)
                elif stage == "OE":
                    act.wait_ge(pv_done, FIRST_STEP[G + 1])
                    if G >= 2:
                        act.wait_ge(bank_full, item("OP", G - 2, 1))
                    a.activation(oT[:, r], pv[r][0:DH + 1, :], copy).then_inc(oT_ready, 1)
                elif stage == "X2T":
                    if G >= 1:
                        act.wait_ge(bank_full, item("LG", G - 1))
                    a.activation(x2T[:, :], ps[:, :], copy).then_inc(bank_act, 1)
                elif stage == "RT":
                    act.wait_ge(gap_ready, G + 1)
                    a.activation(egap[:, :], gap[:, :], ACT.Exp).then_inc(egap_ready, 1)

            def step(base, u, has):
                i = base + u
                if has(1):
                    v = (u + 1) % 2
                    act.wait_ge(h_full, i + 2)
                    wait_count(act, hT_full, i)
                    a.activation(h[:, v], st[0][:, v * F:(v + 1) * F], ACT.Gelu).then_inc(h_ready, 1)
                if has(-1):
                    v, w = (u - 1) % 2, (u - 1) % UN
                    act.wait_ge(y_full, i)
                    a.activation(y[:, w], pv[v][:, 0:D], copy, scale=xg[:, w, D:D + 1]).then_inc(y_ready, 1)

            act.wait_ge(h_full, 1)
            a.activation(h[:, 0], st[0][:, 0:F], ACT.Gelu).then_inc(h_ready, 1)
            expert_rounds(act, step)
            last = NTILE - 1
            act.wait_ge(y_full, NTILE)
            a.activation(y[:, last % UN], pv[last % 2][:, 0:D], copy,
                         scale=xg[:, last % UN, D:D + 1]).then_inc(y_ready, 1)

            for G in range(NG):
                act.wait_ge(out_ready, G + 1)
                act.dma_start(of[G * GQ:(G + 1) * GQ, :].rearrange("(t p) d -> p t d", p=P),
                              xs_[:, G * GT:(G + 1) * GT, :]).then_inc(stored, 16)
            act.wait_ge(stored, 16 * NG)

        @block.vector
        def _(dve):
            v = nc.vector
            links = [0]

            def link(ins):
                links[0] += 1
                ins.then_inc(vec, 1)
                dve.wait_ge(vec, links[0])

            v.memset(wo_aug[DH:DH + 1, D:D + 1], 1.0).then_inc(consts0, 1)
            v.memset(k_h1[DH:DH + 1, :].bitcast(f32), 1.0).then_inc(consts0, 1)

            dve.wait_ge(b_in, 32)
            v.tensor_copy(b_hi[:, :], b_raw[:, :]).then_inc(bias_split, 1)
            dve.wait_ge(bias_split, 1)
            v.tensor_tensor(b_lo[:, :], b_raw[:, :], b_hi[:, :].bitcast(f32), ALU.subtract).then_inc(bias_split, 1)

            def layernorm_stats(G, stats_of, mv_of, veps_of, ready):
                for t in range(GT):
                    ins = v.bn_stats(stats_of[:, t], xs_[:, G * GT + t])
                    if t < GT - 1:
                        ins.then_inc(vec, 1)
                        links[0] += 1
                link(ins)
                for t in range(GT):
                    ins = v.bn_aggr(mv_of[:, t], stats_of[:, t])
                    if t < GT - 1:
                        ins.then_inc(vec, 1)
                        links[0] += 1
                link(ins)
                v.tensor_scalar(veps_of[:, :], mv_of[:, :, 1], EPS, None, ALU.add).then_inc(ready, 1)

            for stage, G, n in SCHEDULE:
                r, cols, tiles = G % 2, slice(G * GQ, (G + 1) * GQ), slice(G * GT, (G + 1) * GT)
                if stage in READERS and "v" in READERS[stage]:
                    dve.wait_ge(bank_full, item(stage, G, n))
                    ps = bank(stage, G, n)
                if stage == "LN1":
                    dve.wait_ge(x_in[G], 16)
                    wait_count(dve, xn_ready, G)
                    wait_count(dve, rstd_ready, G)
                    layernorm_stats(G, stats, mv, veps, var_ready)
                    dve.wait_ge(rstd_ready, G + 1)
                    if G >= 2:
                        dve.wait_ge(bank_full, item("XT", G - 2))
                    for t in range(GT):
                        ins = v.tensor_scalar(xn[:, r, t], xs_[:, G * GT + t], mv[:, t, 0:1], rstd[:, t:t + 1],
                                              ALU.subtract, ALU.mult)
                        if t < GT - 1:
                            ins.then_inc(vec, 1)
                            links[0] += 1
                    ins.then_inc(xn_ready, 1)
                elif stage == "QP":
                    dve.wait_ge(bank_act, ACT_READS[item(stage, G) - 1])
                    if G >= 2:
                        dve.wait_ge(scores_ready, FIRST_STEP[G - 1])
                    v.tensor_tensor(q_lo[0:DH, r], ps[0:DH, :], q_hi[0:DH, r].bitcast(f32),
                                    ALU.subtract).then_inc(bank_dve, 1)
                elif stage == "KP":
                    dve.wait_ge(k_hi_ready, G + 1)
                    v.tensor_tensor(k_hl[DH:P, cols], ps[DH:P, :], k_hl[DH:P, cols].bitcast(f32),
                                    ALU.subtract).then_inc(bank_dve, 1)
                elif stage == "MX":
                    t, c = n
                    g = G % GB
                    if n == (0, 0):
                        wait_count(dve, mneg_ready, G)
                    width = GQ if c < g else (t + 1) * P
                    v.tensor_reduce(mpart[:, t, c:c + 1], ps[:, 0:width], AX.X, ALU.max).then_inc(bank_dve, 1)
                elif stage == "MR":
                    g = G % GB
                    dve.wait_ge(bank_dve, DVE_READS[item("MX", G, (GT - 1, g)) - 1])
                    if G >= 1:
                        dve.wait_ge(bank_full, item("MR", G - 1))
                    else:
                        dve.wait_ge(consts0, N_FILLS)
                    v.tensor_reduce(mneg[:, :, DH], mpart[:, :, 0:g + 1], AX.X, ALU.max,
                                    negate=True).then_inc(mneg_ready, 1)
                elif stage == "OP":
                    both_tiles = ps[:, 0:2 * (D + 1)].rearrange("p (t d) -> p t d", t=2)
                    if G or n:
                        dve.wait_ge(bank_dve, DVE_READS[item("OP", *((G, 0) if n else (G - 1, 1))) - 1])
                    link(v.reciprocal(rsum[:, :], both_tiles[:, :, D]))
                    for t in range(2):
                        tile = G * GT + 2 * n + t
                        if t == 0 and n == 0:
                            dve.wait_ge(xn_ready, G + 1)
                        ins = v.scalar_tensor_tensor(xs_[:, tile], both_tiles[:, t, 0:D], rsum[:, t:t + 1],
                                                     xs_[:, tile], ALU.mult, ALU.add)
                        if t == 0:
                            ins.then_inc(x2_ready, 1)
                    ins.then_inc(bank_dve, 1)
                elif stage == "LN2":
                    dve.wait_ge(bank_dve, DVE_READS[item("OP", G, 1) - 1])
                    dve.wait_ge(x2_ready, 2 * G + 2)
                    wait_count(dve, x2n_ready, G)
                    wait_count(dve, rstd2_ready, G)
                    layernorm_stats(G, stats, mv2, veps2, var2_ready)
                    dve.wait_ge(rstd2_ready, G + 1)
                    if G >= 2:
                        dve.wait_ge(sent[r], 16 * TOP * GT * (G // 2))
                    for t in range(GT):
                        for k in range(TOP):
                            ins = v.tensor_scalar(rows[:, r, t, k, 0:D], xs_[:, G * GT + t], mv2[:, t, 0:1],
                                                  rstd2[:, t:t + 1], ALU.subtract, ALU.mult)
                            if (t, k) != (GT - 1, TOP - 1):
                                ins.then_inc(vec, 1)
                                links[0] += 1
                    ins.then_inc(x2n_ready, 1)
                elif stage == "LG":
                    wait_count(dve, slots_ready, G)
                    v.tensor_copy(lg[:, :, :], ps[:, 0:GT * E].rearrange("p (t e) -> p t e", t=GT)).then_inc(bank_dve, 1)
                    dve.wait_ge(bank_dve, DVE_READS[item("LG", G) - 1])
                    for t in range(GT):
                        link(v.max(top8[:, t], lg[:, t]))
                        link(v.max_index(top_i[:, t], top8[:, t], lg[:, t]))
                    wait_count(dve, egap_ready, G)
                    v.tensor_tensor(gap[:, :], top8[:, :, 1], top8[:, :, 0], ALU.subtract).then_inc(gap_ready, 1)
                    link(v.tensor_copy(top_f[:, :, :], top_i[:, :, 0:TOP]))
                    for k in range(TOP):
                        link(v.tensor_tensor(pick[:, k], expert_id[:, :].unsqueeze(1).to_broadcast((P, GT, E)),
                                             top_f[:, :, k:k + 1].to_broadcast((P, GT, E)), ALU.is_equal))
                    v.tensor_tensor(both[:, :, :], pick[:, 0], pick[:, 1], ALU.add).then_inc(picks_ready, 1)
                elif stage == "RT":
                    dve.wait_ge(egap_ready, G + 1)
                    link(v.tensor_scalar(veps2[:, :], egap[:, :], 1.0, None, ALU.add))
                    link(v.reciprocal(rows[:, r, :, 0, D], veps2[:, :]))
                    link(v.tensor_tensor(rows[:, r, :, 1, D], egap[:, :], rows[:, r, :, 0, D], ALU.mult))
                    link(v.tensor_copy(rows[:, r, :, :, D + 1].bitcast(i32), dest[:, tiles, :]))
                elif stage == "RK":
                    link(v.tensor_copy(rank[:, :, :], ps[:, 0:GT * E].rearrange("p (t e) -> p t e", t=GT)))
                    for k in range(TOP):
                        link(v.tensor_tensor(ranked[:, k], pick[:, k], rank[:, :, :], ALU.mult))
                    link(v.tensor_reduce(slot_f[:, :, :], ranked[:, :, :, :], AX.X, ALU.add))
                    v.scalar_tensor_tensor(slot[:, r], top_f[:, :, :].rearrange("p t k -> p k t"), float(REGION),
                                           slot_f[:, :, :], ALU.mult, ALU.add).then_inc(slots_ready, 1)
                    link(v.tensor_reduce(bothsum[:, :], both[:, :, :].rearrange("p t e -> p e t"), AX.X, ALU.add))
                    link(v.tensor_tensor(seen[:, :], seen[:, :], bothsum[:, :], ALU.add))
                    v.tensor_copy(seen_b[:, :], seen[:, :]).then_inc(bank_dve, 1)
                elif stage == "CN":
                    link(v.tensor_copy(cnt[:, :], ps[:, 0:E]))
                    v.scalar_tensor_tensor(pad_at[:, :], expert_id[:, :], float(REGION), cnt[:, :],
                                           ALU.mult, ALU.add).then_inc(pad_at_ready, 1)
                    link(v.tensor_scalar(cnt_i[:, :], cnt[:, :], float(P - 1), None, ALU.add))
                    link(v.tensor_scalar(nt_i[:, :], cnt_i[:, :], P.bit_length() - 1, None, ALU.logical_shift_right))
                    link(v.tensor_copy(nt_f[:, :], nt_i[:, :]))
                    link(v.tensor_tensor(cum8[:, :, :], incl[:, :, :],
                                         nt_f[:, :].unsqueeze(1).to_broadcast((P, E, E)), ALU.mult))
                    link(v.tensor_reduce(cend[:, :], cum8[:, :, :], AX.X, ALU.add))
                    link(v.tensor_scalar(skip[:, :], nt_f[:, :], -float(P), float(REGION), ALU.mult, ALU.add))
                    link(v.tensor_tensor(past[:, :, :], tile_no[:, :].unsqueeze(2).to_broadcast((P, NTILE, E)),
                                         cend[:, :].unsqueeze(1).to_broadcast((P, NTILE, E)), ALU.is_ge))
                    link(v.tensor_reduce(te_f[:, :], past[:, :, :], AX.X, ALU.add))
                    link(v.tensor_scalar(tile_expert[:, :], te_f[:, :], float(E - 1), None, ALU.min))
                    link(v.tensor_tensor(past2[:, :, :], past[:, :, :],
                                         skip[:, :].unsqueeze(1).to_broadcast((P, NTILE, E)), ALU.mult))
                    link(v.tensor_reduce(tr_f[:, :], past2[:, :, :], AX.X, ALU.add))
                    link(v.scalar_tensor_tensor(te_f[:, :], tile_no[:, :], float(P), tr_f[:, :], ALU.mult, ALU.add))
                    v.tensor_scalar(tile_row[:, :], te_f[:, :], float(E * REGION), None,
                                    ALU.min).then_inc(table_ready, 1)

            def take_xgT(i, par):
                dve.wait_ge(xgT_full, i + 1)
                wait_count(dve, h_full, i - 1)
                v.tensor_copy(xgT[:, par], wk[par][:, 0:P]).then_inc(xgT_ready, 1)

            def step(base, u, has):
                i = base + u
                if has(2):
                    take_xgT(i + 2, u % 2)
                dve.wait_ge(hT_full, i + 1)
                wait_count(dve, y_full, i - 1)
                v.tensor_copy(hT[:, u % 2], st[1][:, (u % 2) * F:(u % 2 + 1) * F]).then_inc(hT_ready, 1)

            take_xgT(0, 0)
            take_xgT(1, 1)
            expert_rounds(dve, step)

            for G in range(NG):
                r, tiles = G % 2, slice(G * GT, (G + 1) * GT)
                dve.wait_ge(yg_in[r], 16 * (G // 2 + 1))
                link(v.tensor_tensor(xs_[:, tiles], xs_[:, tiles], yg[:, r, :, 0:D], ALU.add))
                v.tensor_tensor(xs_[:, tiles], xs_[:, tiles], yg[:, r, :, D:2 * D], ALU.add).then_inc(out_ready, 1)

        @block.tensor
        def _(pe):
            t_ = nc.tensor

            def free_bank(stage, G, n):
                k = ITEM[(stage, G, n)]
                if k >= 2:
                    pe.wait_ge(bank_act, ACT_READS[k - 2])
                    pe.wait_ge(bank_dve, DVE_READS[k - 2])
                return bank(stage, G, n)

            pe.wait_ge(wqkv_in, 112)
            pe.wait_ge(consts, N_CONSTS)
            t_.transpose(st[0][:, 0:P], wq2[:, :], ident[:, :])
            t_.transpose(st[0][:, P:2 * P], wk2[:, :], ident[:, :])
            t_.transpose(st[0][:, 2 * P:2 * P + DH], wv_[:, :], ident[0:DH, 0:DH])
            t_.transpose(st[0][:, 3 * P:4 * P], wo2[:, :], ident[:, :]).then_inc(wT_ready, 1)

            def product_with_v(s):
                G = max(k for k in range(NG) if FIRST_STEP[k] <= s)
                n = s - FIRST_STEP[G]
                pairs = steps(G % GB)
                acc = pv[G % 2]
                pe.wait_ge(probs_ready, s + 1)
                if n == 0 and G >= 2:
                    pe.wait_ge(oT_ready, G - 1)
                for j, (kb, q0, w, col) in enumerate(pairs[n]):
                    ins = t_.matmul(acc[0:DH + 1, q0:q0 + w], V[:, (G // GB) * (S // P) + kb],
                                    prob[:, s % 2, col:col + w], start=(n == 0 and j == 0),
                                    stop=(n == len(pairs) - 1 and j == 1))
                ins.then_inc(pv_done, 1)

            for stage, G, n in SCHEDULE:
                r, b, g = G % 2, G // GB, G % GB
                if stage in READERS:
                    ps = free_bank(stage, G, n)
                if stage == "XT":
                    pe.wait_ge(xn_ready, G + 1)
                    for t in range(GT):
                        ins = t_.transpose(ps[:, t * P:(t + 1) * P], xn[:, r, t], ident[:, :])
                    ins.then_inc(bank_full, 1)
                elif stage in ("QP", "KP"):
                    if stage == "QP":
                        pe.wait_ge(wT_copied, 4)
                        pe.wait_ge(bank_act, ACT_READS[item("XT", G) - 1])
                    t_.matmul(ps[:, :], (wqT if stage == "QP" else wkT)[:, :], xT[:, r], start=True,
                              stop=True).then_inc(bank_full, 1)
                elif stage == "VP":
                    for t in range(GT):
                        ins = t_.matmul(ps[:, t * DH:(t + 1) * DH], xT[:, r, t * P:(t + 1) * P], wvT[:, :],
                                        start=True, stop=True)
                    ins.then_inc(bank_full, 1)
                elif stage == "MX":
                    t, c = n
                    width = GQ if c < g else (t + 1) * P
                    k0 = b * S + c * GQ
                    if n == (0, 0):
                        pe.wait_ge(bank_act, ACT_READS[item("QP", G) - 1])
                        pe.wait_ge(bank_dve, DVE_READS[item("KP", G) - 1])
                    ins = t_.matmul(ps[:, 0:width], q_hi[:, r, t * P:(t + 1) * P], k_hl[:, k0:k0 + width],
                                    start=True, stop=(c < g))
                    if c == g:
                        ins = t_.matmul(ps[:, width - P:width], ident_b[:, :], mask_qk[:, :], start=False, stop=True)
                    ins.then_inc(bank_full, 1)
                elif stage == "MR":
                    pe.wait_ge(mneg_ready, G + 1)
                    for t in range(GT):
                        ins = t_.matmul(ps[0:DH + 1, t * P:(t + 1) * P], mneg[:, t, 0:DH + 1], ident_r[:, :],
                                        start=True, stop=True)
                    ins.then_inc(bank_full, 1)
                elif stage == "AS":
                    s = FIRST_STEP[G] + n
                    if n == 0:
                        pe.wait_ge(bank_act, ACT_READS[item("MR", G) - 1])
                        pe.wait_ge(bank_dve, DVE_READS[item("QP", G) - 1])
                    wait_count(pe, probs_ready, s - 1)
                    for kb, q0, w, col in steps(g)[n]:
                        k0 = b * S + kb * P
                        diagonal = kb >= GT * g
                        o = st[s % 2]
                        t_.matmul(o[:, col:col + w], k_hl[:, k0:k0 + P], q_hi[:, r, q0:q0 + w], start=True, stop=False)
                        ins = t_.matmul(o[:, col:col + w], k_h1[:, k0:k0 + P], q_lo[:, r, q0:q0 + w],
                                        start=False, stop=not diagonal)
                        if diagonal:
                            ins = t_.matmul(o[:, col:col + P], ident_b[:, :], mask_kq[:, :], start=False, stop=True)
                    ins.then_inc(scores_ready, 1)
                    if s:
                        product_with_v(s - 1)
                elif stage == "AE":
                    product_with_v(FIRST_STEP[NG] - 1)
                elif stage == "OP":
                    pe.wait_ge(oT_ready, G + 1)
                    pe.wait_ge(wout_in, 16)
                    for t in range(2):
                        q0 = (2 * n + t) * P
                        ins = t_.matmul(ps[:, t * (D + 1):(t + 1) * (D + 1)], oT[:, r, q0:q0 + P], wo_aug[:, :],
                                        start=True, stop=True)
                    ins.then_inc(bank_full, 1)
                elif stage == "X2T":
                    pe.wait_ge(x2n_ready, G + 1)
                    for t in range(GT):
                        ins = t_.transpose(ps[:, t * P:(t + 1) * P], rows[:, r, t, 0, 0:D], ident[:, :])
                    ins.then_inc(bank_full, 1)
                elif stage == "LG":
                    pe.wait_ge(gate_in, 16)
                    pe.wait_ge(bank_act, ACT_READS[item("X2T", G) - 1])
                    for t in range(GT):
                        ins = t_.matmul(ps[:, t * E:(t + 1) * E], x2T[:, t * P:(t + 1) * P], gate[:, :],
                                        start=True, stop=True)
                    ins.then_inc(bank_full, 1)
                elif stage == "RK":
                    pe.wait_ge(picks_ready, G + 1)
                    if G >= 1:
                        pe.wait_ge(bank_dve, DVE_READS[item("RK", G - 1) - 1])
                    for t in range(GT):
                        o = ps[:, t * E:(t + 1) * E]
                        t_.matmul(o, ones_b[:, :], seen_b[:, :], start=True, stop=False)
                        for t2 in range(t):
                            t_.matmul(o, ones_b[:, :], both[:, t2], start=False, stop=False)
                        ins = t_.matmul(o, tri[:, :], both[:, t], start=False, stop=True)
                    ins.then_inc(bank_full, 1)
                elif stage == "CN":
                    pe.wait_ge(bank_dve, DVE_READS[item("RK", NG - 1) - 1])
                    t_.matmul(ps[:, 0:E], ones_b[:, :], seen_b[:, :], start=True, stop=True).then_inc(bank_full, 1)

            def transpose_rows(base, k):
                pe.wait_ge(xg_in[k % UN], 4 * base + 16 * (k // UN + 1))
                wait_count(pe, xgT_ready, base + k - 1)
                t_.transpose(wk[k % 2][:, 0:P], xg[:, k % UN, 0:D], ident[:, :]).then_inc(xgT_full, 1)

            def expert(i):
                return pe.value_load(tile_expert[0:1, bass.ds(i, 1)], min_val=0, max_val=E - 1)

            def first_product(base, k):
                e = expert(base + k)
                pe.wait_ge(xgT_ready, base + k + 1)
                wait_count(pe, h_ready, base + k - 1)
                o = st[0][:, (k % 2) * F:(k % 2 + 1) * F]
                t_.matmul(o, xgT[:, k % 2], w1_sb[:, bass.ds(e * F, F)], start=True, stop=False)
                t_.matmul(o, ones_r[:, :], b1_r[:, bass.ds(e * F, F)], start=False, stop=True).then_inc(h_full, 1)

            def second_product(base, k):
                e = expert(base + k)
                pe.wait_ge(hT_ready, base + k + 1)
                wait_count(pe, y_ready, base + k - 1)
                o = pv[k % 2][:, 0:D]
                for c in range(FC):
                    t_.matmul(o, hT[:, k % 2, c * P:(c + 1) * P], w2_sb[:, bass.ds(e * F + c * D, D)],
                              start=(c == 0), stop=False)
                t_.matmul(o, ones_r[:, :], b2_r[:, bass.ds(e * D, D)], start=False, stop=True).then_inc(y_full, 1)

            def step(base, u, has):
                if has(1):
                    first_product(base, u + 1)
                if has(-1):
                    second_product(base, u - 1)
                if has(2):
                    transpose_rows(base, u + 2)
                pe.wait_ge(h_ready, base + u + 1)
                wait_count(pe, hT_ready, base + u - 1)
                for c in range(FC):
                    o = (u % 2) * F + c * P
                    ins = t_.transpose(st[1][:, o:o + P], h[:, u % 2, c * P:(c + 1) * P], ident[:, :])
                ins.then_inc(hT_full, 1)

            pe.wait_ge(table_ready, 1)
            pe.wait_ge(w12_in, 32)
            pe.wait_ge(bias_in, 64)
            transpose_rows(0, 0)
            transpose_rows(0, 1)
            first_product(0, 0)
            expert_rounds(pe, step)
            second_product(NTILE - UN, UN - 1)


_INS = ['L0_attn_x', 'L0_attn_w_qkv', 'L0_attn_w_out', 'L0_attn_b_out', 'L0_ffn_gate_w',
        'L0_ffn_w1', 'L0_ffn_b1', 'L0_ffn_w2', 'L0_ffn_b2']
_OUTS = [((2, 2048, 128), 'float32')]


def kernel(**inputs):
    import numpy as _np
    import concourse.bacc as _bacc
    from concourse import mybir as _mybir
    from concourse.bass_utils import run_bass_kernel_spmd as _run

    nc = _bacc.Bacc("TRN2", target_bir_lowering=False, num_devices=1)
    arrays, args = {}, []
    for name in _INS:
        a = _np.ascontiguousarray(inputs[name])
        arrays[f"in_{name}_dram"] = a
        args.append(nc.dram_tensor(f"in_{name}_dram", a.shape, _mybir.dt.from_np(a.dtype), kind="ExternalInput").ap())
    for i, (shape, dtype) in enumerate(_OUTS):
        dt = _mybir.dt.from_np(_np.dtype(dtype))
        args.append(nc.dram_tensor(f"out_{i}_dram", shape, dt, kind="ExternalOutput").ap())
    preln_attention_moe(nc, *args)
    r = _run(nc, [arrays], core_ids=[0])
    return r.results[0]["out_0_dram"]
```

```python
import concourse.bass as bass
from concourse import mybir
from contextlib import ExitStack


def preln_attention_moe(nc, x, w_qkv, w_out, b_out, gate_w, w1, b1, w2, b2, out):
    f32, f32r, bf16 = mybir.dt.float32, mybir.dt.float32r, mybir.dt.bfloat16
    i32, u32 = mybir.dt.int32, mybir.dt.uint32
    ALU, ACT, AX = mybir.AluOpType, mybir.ActivationFunctionType, mybir.AxisListType

    P = 128
    B, S, D = x.shape
    DH = w_out.shape[1]
    E, _, F = w1.shape
    TOP = 2
    T = B * S
    NT = T // P
    GT = 4
    GQ = GT * P
    NG = NT // GT
    GB = S // GQ
    FC = F // P
    SCALE = float(DH) ** -0.5
    EPS = 1e-5
    NEG = -1e38
    REGION = T + P
    ROW = D + 2
    NSLOT = T * TOP
    MAXT = NSLOT // P + E - 1
    UN = 8
    KR, VR = 6, 6
    QR = 3
    LAG = 3
    ACT_DELAY, DVE_DELAY = 0.2, 0.32
    PR, BR = LAG + 1, 3
    NTILE = -(-MAXT // UN) * UN
    FAR = 1 << 20

    N_FILLS, N_CONSTS = 22, 9

    xf = x.rearrange("b n d -> (b n) d")
    of = out.rearrange("b n d -> (b n) d")
    disp = nc.dram_tensor("dispatched_rows", (E * REGION + P, ROW), f32, kind="Internal").ap()
    ys = nc.dram_tensor("expert_results", (NSLOT, D), f32, kind="Internal").ap()

    def steps(g):
        return [(kb, max(0, kb - GT * g) * P, GQ - max(0, kb - GT * g) * P) for kb in range(GT * (g + 1))]

    FIRST_STEP = [0]
    for G in range(NG):
        FIRST_STEP.append(FIRST_STEP[-1] + len(steps(G % GB)))

    PACE = 0.58
    LEAD, TO_NORM = 5.78, 0.9
    TO_MR, MR_TO_STEP = 1.0, 0.6
    TO_BACK = 0.5
    TO_SC, SC_PACE = 1.0, 1.1
    BACK_AT = (("OP", 0, 1.0), ("OP", 1, 1.88), ("LN2", 0, 2.88), ("NORM2", 0, 3.88), ("X2T", 0, 5.63),
               ("LG", 0, 7.19), ("RT", 0, 8.19), ("RK", 0, 10.11))
    timed = [(s, 0, ("AS", G, s - FIRST_STEP[G])) for G in range(NG) for s in range(FIRST_STEP[G], FIRST_STEP[G + 1])]
    timed += [(FIRST_STEP[NG] + n, 0, ("AE", NG - 1, n)) for n in range(LAG)]
    start, xt_at = FIRST_STEP[NG], {}
    for G in reversed(range(NG)):
        parts = [("XT", 0), ("QP", 0), ("KP", 0), ("VP", 0)] + [("MX", (t, c)) for t in range(GT) for c in range(G % GB + 1)]
        last = min(start, FIRST_STEP[G] - MR_TO_STEP - TO_MR)
        timed.append((last + TO_MR, 1, ("MR", G, 0)))
        start = max(last - PACE * len(parts), -2.0 if G == 0 else -1.2)
        timed += [(start + (last - start) * i / len(parts), 1, (part, G, n)) for i, (part, n) in enumerate(parts)]
        xt_at[G] = start
    norm = -9
    for G in range(NG):
        ln = max(xt_at[G] - LEAD, norm + 0.1)
        norm = max(ln + TO_NORM, xt_at[G - 2] + 0.5 if G >= 2 else norm)
        timed += [(ln, 1, ("LN1", G, 0)), (norm, 1, ("NORM1", G, 0))]
        assert norm < xt_at[G]
    end = 0
    for G in range(NG):
        begin = FIRST_STEP[G + 1] + LAG - TO_BACK
        timed.append((begin, 2, ("OE", G, 0)))
        begin = max(end, begin)
        timed += [(begin + after, 2, (part, G, n)) for part, n, after in BACK_AT]
        end = begin + BACK_AT[-1][2]
        timed += [(end + TO_SC + SC_PACE * t, 2, ("SC", G, t)) for t in range(GT)]
        timed.append((FIRST_STEP[G] + 1.4, 3, ("WS", G, 0)))
    timed.append((end + 1, 3, ("CN", NG - 1, 0)))

    def order(delay):
        at = sorted((t + (delay if part[0] not in ("AS", "AE", "OE", "SC") else 0), k, t, part) for t, k, part in timed)
        return [part for _, _, _, part in at]

    SCHEDULE, ACT_ORDER, DVE_ORDER = order(0), order(ACT_DELAY), order(DVE_DELAY)

    READERS = {"XT": "a", "QP": "av", "KP": "av", "VP": "av", "MX": "v", "MR": "a",
               "OP": "v", "X2T": "a", "LG": "v", "RK": "v", "CN": "v"}
    ITEM, ACT_READS, DVE_READS = {}, [], []
    for part in SCHEDULE:
        if part[0] in READERS:
            who = READERS[part[0]]
            ITEM[part] = len(ITEM)
            ACT_READS.append((ACT_READS[-1] if ACT_READS else 0) + ("a" in who))
            DVE_READS.append((DVE_READS[-1] if DVE_READS else 0) + ("v" in who))

    ctx = ExitStack()
    with ctx:
        def sb(name, shape, dt=f32):
            return ctx.enter_context(nc.sbuf_tensor(name, shape, dt))

        def pb(name, shape, dt=f32):
            return ctx.enter_context(nc.psum_tensor(name, shape, dt))

        def sem(name):
            return ctx.enter_context(nc.semaphore(name))

        ident = sb("ident", [P, P])
        ident_r = sb("ident_r", [P, P], f32r)
        ident_b = sb("ident_b", [P, P], bf16)
        mask_kq = sb("mask_kq", [P, P], bf16)
        mask_qk = sb("mask_qk", [P, P], bf16)
        tri = sb("tri", [P, P], bf16)
        ones_b = sb("ones_b", [P, P], bf16)
        sum_col = sb("sum_col", [P, DH + 1], f32r)
        mhalf = sb("mhalf", [P, GT])
        expert_id = sb("expert_id", [P, E])
        dest = sb("dest", [P, NT, TOP], i32)
        tile_no_i = sb("tile_no_i", [P, NTILE], i32)
        expert_i = sb("expert_i", [P, E], i32)
        tile_no = sb("tile_no", [P, NTILE])
        incl = sb("incl", [P, E, E])
        wq_dup, wk_dup, wv_ = sb("wq_dup", [P, D]), sb("wk_dup", [P, D]), sb("wv_", [DH, D])
        wo2 = sb("wo2", [P, 2 * DH])
        wqT, wkT, wvT = sb("wqT", [D, P]), sb("wkT", [D, P]), sb("wvT", [D, DH])
        wo_dup = sb("wo_dup", [P, D + 1])
        wo_aug = sb("wo_aug", [DH + 1, D + 1])
        gate = sb("gate", [D, E])
        w_raw = sb("w_raw", [P, 2, F])
        w1p = sb("w1p", [P, E, 2, F], f32r)
        w2p = sb("w2p", [P, E, FC, 2, D], f32r)
        NB, NB1, NB2 = 3, E * F // P, E * D // P
        b_raw = sb("b_raw", [P, NB1 + NB2])
        b_part = sb("b_part", [P, NB, NB1 + NB2], bf16)
        b1_r = sb("b1_r", [NB, E * F], bf16)
        b2_r = sb("b2_r", [NB, E * D], bf16)
        xs_ = sb("xs_", [P, NT, D])
        stats = sb("stats", [P, GT, 6])
        mv = sb("mv", [P, GT, 2])
        veps = sb("veps", [P, GT])
        rstd = sb("rstd", [P, GT])
        mv2 = sb("mv2", [P, GT, 2])
        veps2 = sb("veps2", [P, GT])
        rstd2 = sb("rstd2", [P, GT])
        xn2 = sb("xn", [P, 2, GT * D])
        xn = xn2[:, :, :].rearrange("p r (t d) -> p r t d", t=GT)
        xT = sb("xT", [D, 2, GQ])
        q_hi = sb("q_hi", [P, QR, GQ], f32r)
        q_lo = sb("q_lo", [DH + 1, QR, GQ], f32r)
        k_hl = sb("k_hl", [P, KR * GQ], f32r)
        k_h1 = sb("k_h1", [DH + 1, KR * GQ], f32r)
        V = sb("V", [P, VR * GT, 2 * DH + 2], f32r)
        mpart = sb("mpart", [P, GT, GB])
        mneg = sb("mneg", [P, GT, DH + 2], f32r)
        prob = sb("prob", [P, 2, GQ])
        p_hi = sb("p_hi", [P, PR, GQ], f32r)
        p_lo = sb("p_lo", [P, PR, GQ], f32r)
        oA = sb("oA", [P, GQ])
        oB = sb("oB", [DH + 1, GQ])
        rsum = sb("rsum", [P, 2])
        rows = sb("rows", [P, 2, GT, TOP, ROW])
        x2T = sb("x2T", [D, GQ])
        lg = sb("lg", [P, GT, E])
        top8 = sb("top8", [P, GT, 8])
        top_i = sb("top_i", [P, GT, 8], u32)
        top_f = sb("top_f", [P, GT, TOP])
        pick = sb("pick", [P, TOP, GT, E])
        both = sb("both", [P, GT, E], bf16)
        bothsum = sb("bothsum", [P, E])
        seen = sb("seen", [P, E])
        seen_b = sb("seen_b", [P, E], bf16)
        gap = sb("gap", [P, GT])
        egap = sb("egap", [P, GT])
        rank = sb("rank", [P, GT, E])
        ranked = sb("ranked", [P, TOP, GT, E])
        slot_f = sb("slot_f", [P, TOP, GT])
        slot = sb("slot", [P, 2, TOP, GT], u32)
        cnt = sb("cnt", [P, E])
        cnt_i = sb("cnt_i", [P, E], i32)
        pad_at = sb("pad_at", [P, E], i32)
        nt_i = sb("nt_i", [P, E], i32)
        nt_f = sb("nt_f", [P, E])
        cum8 = sb("cum8", [P, E, E])
        cend = sb("cend", [P, E])
        skip = sb("skip", [P, E])
        past = sb("past", [P, NTILE, E])
        past2 = sb("past2", [P, NTILE, E])
        te_f = sb("te_f", [P, NTILE])
        tr_f = sb("tr_f", [P, NTILE])
        tile_expert = sb("tile_expert", [P, NTILE], i32)
        tile_row = sb("tile_row", [P, NTILE], i32)
        pad_rows = sb("pad_rows", [P, ROW])
        meta = sb("meta", [P, UN, 2])
        XR = 4
        xg = rows[:, 0].rearrange("p t k n -> p (t k) n")
        xgT_hi, xgT_lo = (q_hi[:, i].rearrange("p (i n) -> p i n", i=XR) for i in range(2))
        h = prob[:, :, :]
        y = w_raw[:, :, :].rearrange("p a (i d) -> p (a i) d", d=D)
        hT_hi = k_hl[:, 0:XR * F].rearrange("p (i f) -> p i f", i=XR)
        hT_lo = p_hi[:, 0:XR]
        yg = [b[:, :].rearrange("p a n -> p (a n)").rearrange("p (t d) -> p t d", t=GT) for b in (xn2, xT, prob, w_raw)]
        yg += [rows[:, i].rearrange("p t k n -> p (t k n)")[:, 0:TOP * GT * D].rearrange("p (t d) -> p t d", t=GT)
               for i in range(2)]

        st = [pb(f"st{i}", [P, GQ]) for i in range(BR)]
        pv = [pb(f"pv{i}", [P, GQ]) for i in range(2)]
        wk = [pb(f"wk{i}", [P, GQ]) for i in range(BR)]
        h_ps, hT_ps = st[0:2], (st[2], wk[2])

        x_in = [sem(f"x_in{G}") for G in range(NG)]
        wqkv_in, wout_in, gate_in, w12_in = sem("wqkv_in"), sem("wout_in"), sem("gate_in"), sem("w12_in")
        w_hi_ready, w_lo_ready = sem("w_hi_ready"), sem("w_lo_ready")
        b_in, bias_split, bias_in = sem("b_in"), sem("bias_split"), sem("bias_in")
        consts0, consts = sem("consts0"), sem("consts")
        wT_ready, wT_copied = sem("wT_ready"), sem("wT_copied")
        vec = sem("vec")
        var_ready, rstd_ready = sem("var_ready"), sem("rstd_ready")
        xn_ready, xT_ready = sem("xn_ready"), sem("xT_ready")
        q_hi_ready, q_lo_ready = sem("q_hi_ready"), sem("q_lo_ready")
        k_hi_ready = sem("k_hi_ready")
        mneg_ready, mrow_ready = sem("mneg_ready"), sem("mrow_ready")
        bank_full, bank_act, bank_dve = sem("bank_full"), sem("bank_act"), sem("bank_dve")
        scores_ready, probs_ready, pv_done = sem("scores_ready"), sem("probs_ready"), sem("pv_done")
        p_hi_ready, p_lo_ready, v_hi_ready = sem("p_hi_ready"), sem("p_lo_ready"), sem("v_hi_ready")
        oT_ready, x2_ready = sem("oT_ready"), sem("x2_ready")
        var2_ready, rstd2_ready = sem("var2_ready"), sem("rstd2_ready")
        x2n_ready, x2T_ready = sem("x2n_ready"), sem("x2T_ready")
        gap_ready, egap_ready, picks_ready = sem("gap_ready"), sem("egap_ready"), sem("picks_ready")
        slots_ready = sem("slots_ready")
        sent = [sem(f"sent{i}") for i in range(2)]
        counts_ready, pad_at_ready, table_ready, padded = (sem("counts_ready"), sem("pad_at_ready"),
                                                           sem("table_ready"), sem("padded"))
        xg_in = [sem(f"xg_in{u}") for u in range(UN)]
        xgT_full, xgT_hi_ready, xgT_ready = sem("xgT_full"), sem("xgT_hi_ready"), sem("xgT_ready")
        meta_ready, hT_hi_ready = sem("meta_ready"), sem("hT_hi_ready")
        h_full, h_ready = sem("h_full"), sem("h_ready")
        hT_full, hT_ready = sem("hT_full"), sem("hT_ready")
        y_full, y_ready = sem("y_full"), sem("y_ready")
        y_rest_ready = sem("y_rest_ready")
        scatters_begun = sem("scatters_begun")
        y_sent = [sem(f"y_sent{u}") for u in range(UN)]
        yg_in = [sem(f"yg_in{G}") for G in range(NG)]
        out_ready, stored = sem("out_ready"), sem("stored")

        block = ctx.enter_context(nc.Block())

        def item(stage, G, n=0):
            return ITEM[(stage, G, n)] + 1

        def bank(stage, G, n=0):
            return wk[ITEM[(stage, G, n)] % BR]

        def keys_of(G):
            return slice(G % KR * GQ, (G % KR + 1) * GQ)

        def values_of(G):
            return slice(G % VR * GT, (G % VR + 1) * GT)

        def values_at(G, kb):
            return (G // GB * GB + kb // GT) % VR * GT + kb % GT

        def wait_count(eng, semaphore, n):
            if not (isinstance(n, int) and n <= 0):
                eng.wait_ge(semaphore, n)

        def expert_rounds(eng, step):
            for u in range(UN):
                step(0, u, lambda k: u + k >= 0)
            with eng.Fori(1, NTILE // UN - 1) as turn:
                for u in range(UN):
                    step(turn * UN, u, lambda k: True)
            for u in range(UN):
                step(NTILE - UN, u, lambda k: u + k < UN)

        def yload(G):
            return ys[G * GQ * TOP:(G + 1) * GQ * TOP, :].rearrange("(t p k) d -> p t (k d)", p=P, k=TOP)

        @block.sync
        def _(sp):
            for G in range(NG):
                sp.dma_start(xs_[:, G * GT:(G + 1) * GT, :],
                             xf[G * GQ:(G + 1) * GQ, :].rearrange("(t p) d -> p t d", p=P)).then_inc(x_in[G], 16)
                if G == 0:
                    for i in range(2):
                        sp.dma_start(wq_dup[i * DH:(i + 1) * DH, :], w_qkv[0:DH, :]).then_inc(wqkv_in, 16)
                        sp.dma_start(wk_dup[i * DH:(i + 1) * DH, :], w_qkv[DH:2 * DH, :]).then_inc(wqkv_in, 16)
                    sp.dma_start(wv_[:, :], w_qkv[2 * DH:3 * DH, :]).then_inc(wqkv_in, 16)
                    sp.dma_start(wo2[:, 0:DH], w_out).then_inc(wqkv_in, 16)
                    sp.dma_start(wo2[:, DH:], w_out).then_inc(wqkv_in, 16)
                    sp.dma_start(wo_aug[DH:DH + 1, 0:D], b_out.rearrange("(a n) -> a n", a=1)).then_inc(wout_in, 16)
                    sp.dma_start(gate[:, :], gate_w).then_inc(gate_in, 16)
                    sp.dma_start(b_raw[:, 0:NB1], b1.rearrange("e f -> (e f)").rearrange("(p n) -> p n", p=P)).then_inc(b_in, 16)
                    sp.dma_start(b_raw[:, NB1:], b2.rearrange("e d -> (e d)").rearrange("(p n) -> p n", p=P)).then_inc(b_in, 16)
            sp.wait_ge(bias_split, 2 * NB - 1)
            for i in range(NB):
                sp.dma_start(b1_r[i:i + 1, :], b_part[:, i, 0:NB1]).then_inc(bias_in, 16)
                sp.dma_start(b2_r[i:i + 1, :], b_part[:, i, NB1:]).then_inc(bias_in, 16)
            for e in range(E):
                wait_count(sp, w_hi_ready, 2 * e)
                wait_count(sp, w_lo_ready, 2 * e)
                sp.dma_start(w_raw[:, 0, :], w1[e, :, :]).then_inc(w12_in, 16)
                sp.dma_start(w_raw[:, 1, :].rearrange("p (c d) -> p c d", c=FC),
                             w2[e, :, :].rearrange("(c p) d -> p c d", p=P)).then_inc(w12_in, 16)
            sp.wait_ge(consts0, N_FILLS)
            sp.dma_start(disp[E * REGION:E * REGION + P, :], pad_rows[:, :]).then_inc(padded, 16)
            sp.wait_ge(pad_at_ready, 1)
            for at in [sp.value_load(pad_at[0:1, e:e + 1], min_val=e * REGION, max_val=e * REGION + T) for e in range(E)]:
                sp.dma_start(disp[bass.ds(at, P), :], pad_rows[:, :]).then_inc(padded, 16)

            def first_row(i):
                return sp.value_load(tile_row[0:1, bass.ds(i, 1)], min_val=0, max_val=E * REGION)

            sp.wait_ge(table_ready, 1)
            first_rows = [first_row(u) for u in range(UN)]
            for i in range(2):
                sp.wait_ge(sent[i], 16 * TOP * GT * (NG // 2))
            sp.wait_ge(padded, 16 * (E + 1))

            def load_rows(base, u):
                at = first_rows[u] if isinstance(base, int) else first_row(base + u)
                wait_count(sp, meta_ready, base + (u + 1 - UN))
                wait_count(sp, xgT_full, base + (u + 1 - UN))
                sp.dma_start(xg[:, u, :], disp[bass.ds(at, P), :]).then_inc(xg_in[u], 16)

            for u in range(UN):
                load_rows(0, u)
            with sp.Fori(1, NTILE // UN) as turn:
                for u in range(UN):
                    load_rows(turn * UN, u)

            for u in range(UN):
                sp.wait_ge(y_sent[u], 16 * (NTILE // UN))
            for G in range(NG):
                if G >= len(yg):
                    sp.wait_ge(out_ready, G - len(yg) + 1)
                sp.dma_start(yg[G % len(yg)], yload(G)).then_inc(yg_in[G], 16)

        @block.gpsimd
        def _(pool):
            g = nc.gpsimd
            g.memset(wo_aug[0:DH, D:D + 1], 0.0).then_inc(consts0, 1)
            g.memset(ident[:, :], 0.0).then_inc(consts0, 1)
            g.memset(mask_kq[:, :], 0.0).then_inc(consts0, 1)
            g.memset(mask_qk[:, :], 0.0).then_inc(consts0, 1)
            g.memset(tri[:, :], 1.0).then_inc(consts0, 1)
            g.memset(incl[:, :, :], 1.0).then_inc(consts0, 1)
            g.memset(ones_b[:, :], 1.0).then_inc(consts0, 1)
            g.memset(sum_col[:, 0:DH].bitcast(f32), 0.0).then_inc(consts0, 1)
            g.memset(sum_col[:, DH:DH + 1].bitcast(f32), 1.0).then_inc(consts0, 1)
            g.memset(wo_dup[:, D:D + 1], 0.0).then_inc(consts0, 1)
            g.memset(mhalf[:, :], -0.5).then_inc(consts0, 1)
            g.memset(mneg[:, :, :].bitcast(f32), 0.0).then_inc(consts0, 1)
            g.memset(V[:, :, 2 * DH:].bitcast(f32), 1.0).then_inc(consts0, 1)
            g.memset(seen[:, :], 0.0).then_inc(consts0, 1)
            g.memset(seen_b[:, :], 0.0).then_inc(consts0, 1)
            g.memset(pad_rows[:, 0:D + 1], 0.0).then_inc(consts0, 1)
            g.memset(pad_rows[:, D + 1:ROW].bitcast(i32), FAR).then_inc(consts0, 1)
            g.iota(tile_no_i[:, :], [[1, NTILE]], base=0, channel_multiplier=0).then_inc(consts0, 1)
            g.iota(expert_i[:, :], [[1, E]], base=0, channel_multiplier=0).then_inc(consts0, 1)
            g.iota(dest[:, :, :], [[TOP * P, NT], [1, TOP]], base=0, channel_multiplier=TOP).then_inc(consts0, 1)
            pool.wait_ge(consts0, N_FILLS)
            g.affine_select(out=ident[:, :], in_=ident[:, :], compare_op=ALU.not_equal, fill=1.0, base=0,
                            pattern=[[-1, P]], channel_multiplier=1).then_inc(consts, 1)
            g.affine_select(out=mask_kq[:, :], in_=mask_kq[:, :], compare_op=ALU.is_ge, fill=NEG, base=0,
                            pattern=[[1, P]], channel_multiplier=-1).then_inc(consts, 1)
            g.affine_select(out=mask_qk[:, :], in_=mask_qk[:, :], compare_op=ALU.is_ge, fill=NEG, base=0,
                            pattern=[[-1, P]], channel_multiplier=1).then_inc(consts, 1)
            g.affine_select(out=tri[:, :], in_=tri[:, :], compare_op=ALU.is_gt, fill=0.0, base=0,
                            pattern=[[1, P]], channel_multiplier=-1).then_inc(consts, 1)
            g.affine_select(out=incl[:, :, :], in_=incl[:, :, :], compare_op=ALU.is_ge, fill=0.0, base=0,
                            pattern=[[1, E], [-1, E]], channel_multiplier=0).then_inc(consts, 1)
            g.tensor_copy(tile_no[:, :], tile_no_i[:, :]).then_inc(consts, 1)
            g.tensor_copy(expert_id[:, :], expert_i[:, :]).then_inc(consts, 1)
            pool.wait_ge(consts, 1)
            g.tensor_copy(ident_r[:, :], ident[:, :]).then_inc(consts, 1)
            g.tensor_copy(ident_b[:, :], ident[:, :]).then_inc(consts, 1)

            for stage, G, n in SCHEDULE:
                r = G % 2
                if stage == "LN1":
                    pool.wait_ge(var_ready, G + 1)
                    wait_count(pool, xn_ready, G)
                    g.tensor_tensor(rstd[:, :], veps[:, :], mhalf[:, :], ALU.pow).then_inc(rstd_ready, 1)
                elif stage == "LN2":
                    pool.wait_ge(var2_ready, G + 1)
                    wait_count(pool, x2n_ready, G)
                    g.tensor_tensor(rstd2[:, :], veps2[:, :], mhalf[:, :], ALU.pow).then_inc(rstd2_ready, 1)
                elif stage == "WS":
                    pool.wait_ge(w_hi_ready, 2 * (G + 1))
                    g.tensor_tensor(w1p[:, G, 1], w_raw[:, 0], w1p[:, G, 0].bitcast(f32),
                                    ALU.subtract).then_inc(w_lo_ready, 1)
                    g.tensor_tensor(w2p[:, G, :, 1], w_raw[:, 1].rearrange("p (c d) -> p c d", c=FC),
                                    w2p[:, G, :, 0].bitcast(f32), ALU.subtract).then_inc(w_lo_ready, 1)
                elif stage == "SC":
                    if n == 0:
                        pool.wait_ge(slots_ready, G + 1)
                    for k in range(TOP):
                        g.indirect_dma_start(
                            out=disp, out_offset=bass.IndirectOffsetOnAxis(ap=slot[:, r, k, n:n + 1], axis=0),
                            in_=rows[:, r, n, k, :], in_offset=None).then_inc(sent[r], 16)

            bound = pool.to_reg(NSLOT - 1)

            def step(base, u, has):
                pool.wait_ge(y_ready, base + u + 1)
                pool.sem_inc(scatters_begun, 1)
                g.indirect_dma_start(
                    out=ys, out_offset=bass.IndirectOffsetOnAxis(ap=meta[:, u, 1:2].bitcast(u32), axis=0),
                    in_=y[:, u, :], in_offset=None, bounds_check=bound, oob_is_err=False).then_inc(y_sent[u], 16)

            expert_rounds(pool, step)

        @block.scalar
        def _(act):
            a = nc.scalar
            copy = ACT.Copy
            act.wait_ge(wT_ready, 1)
            a.activation(wqT[:, :], st[0][:, 0:P], copy).then_inc(wT_copied, 1)
            a.activation(wkT[:, :], st[0][:, P:2 * P], copy).then_inc(wT_copied, 1)
            a.activation(wvT[:, :], st[0][:, 2 * P:2 * P + DH], copy).then_inc(wT_copied, 1)
            a.activation(wo_aug[0:DH, 0:D], st[0][0:DH, 3 * P:4 * P], copy).then_inc(wT_copied, 1)
            a.activation(wo_dup[:, 0:D], st[0][:, 3 * P:4 * P], copy).then_inc(wT_copied, 1)

            for stage, G, n in ACT_ORDER:
                r, cols = G % 2, slice(G * GQ, (G + 1) * GQ)
                if stage in READERS and "a" in READERS[stage]:
                    act.wait_ge(bank_full, item(stage, G, n))
                    ps = bank(stage, G, n)
                if stage == "XT":
                    if G >= 2:
                        act.wait_ge(bank_full, item("VP", G - 2))
                    a.activation(xT[:, r], ps[:, :], copy).then_inc(bank_act, 1)
                elif stage == "QP":
                    if G >= QR:
                        act.wait_ge(scores_ready, FIRST_STEP[G - QR + 1])
                    a.activation(q_hi[:, G % QR], ps[:, :], copy).then_inc(bank_act, 1)
                elif stage == "KP":
                    if G >= KR:
                        act.wait_ge(scores_ready, FIRST_STEP[GB])
                    a.activation(k_hl[:, keys_of(G)], ps[:, :], copy).then_inc(k_hi_ready, 1)
                    a.activation(k_h1[0:DH, keys_of(G)], ps[0:DH, :], copy).then_inc(bank_act, 1)
                elif stage == "VP":
                    if G >= VR:
                        act.wait_ge(pv_done, FIRST_STEP[GB])
                    a.activation(V[:, values_of(G), DH:2 * DH],
                                 ps[:, 0:GT * DH].rearrange("p (t d) -> p t d", t=GT), copy).then_inc(bank_act, 1)
                elif stage == "WS":
                    act.wait_ge(w12_in, 32 * (G + 1))
                    a.activation(w1p[:, G, 0], w_raw[:, 0], copy).then_inc(w_hi_ready, 1)
                    a.activation(w2p[:, G, :, 0], w_raw[:, 1].rearrange("p (c d) -> p c d", c=FC),
                                 copy).then_inc(w_hi_ready, 1)
                elif stage == "MR":
                    if G >= QR:
                        act.wait_ge(scores_ready, FIRST_STEP[G - QR + 1])
                    a.activation(q_lo[DH:DH + 1, G % QR, :], ps[DH:DH + 1, :], copy).then_inc(bank_act, 1)
                elif stage == "AS":
                    s = FIRST_STEP[G] + n
                    act.wait_ge(scores_ready, s + 1)
                    wait_count(act, p_lo_ready, s - 1)
                    width = steps(G % GB)[n][2]
                    a.activation(prob[:, s % 2, 0:width], st[s % BR][:, 0:width], ACT.Exp,
                                 scale=SCALE).then_inc(probs_ready, 1)
                    wait_count(act, pv_done, s - PR + 1)
                    a.activation(p_hi[:, s % PR, 0:width], st[s % BR][:, 0:width], ACT.Exp,
                                 scale=SCALE).then_inc(p_hi_ready, 1)
                elif stage == "OE":
                    act.wait_ge(pv_done, FIRST_STEP[G + 1])
                    if G >= 1:
                        act.wait_ge(bank_full, item("OP", G - 1, 1))
                    a.activation(oA[:, :], pv[0][:, :], copy).then_inc(oT_ready, 1)
                    a.activation(oB[:, :], pv[1][0:DH + 1, :], copy).then_inc(oT_ready, 1)
                elif stage == "X2T":
                    if G >= 1:
                        act.wait_ge(bank_full, item("LG", G - 1))
                    a.activation(x2T[:, :], ps[:, :], copy).then_inc(bank_act, 1)
                elif stage == "RT":
                    act.wait_ge(gap_ready, G + 1)
                    a.activation(egap[:, :], gap[:, :], ACT.Exp).then_inc(egap_ready, 1)

            def take_gelu(base, k):
                act.wait_ge(h_full, base + k + 1)
                wait_count(act, hT_full, base + (k - 1))
                a.activation(h[:, k % 2], h_ps[k % 2][:, :], ACT.Gelu).then_inc(h_ready, 1)

            def weigh(base, k):
                act.wait_ge(y_full, base + k + 1)
                a.activation(y[:, k % UN], pv[k % 2][:, D:2 * D], copy,
                             scale=meta[:, k % UN, 0:1]).then_inc(y_rest_ready, 1)

            def step(base, u, has):
                if has(1):
                    take_gelu(base, u + 1)
                if has(-2):
                    weigh(base, u - 2)
                act.wait_ge(hT_full, base + u + 1)
                wait_count(act, y_full, base + (u + 1 - XR))
                a.activation(hT_hi[:, u % XR], hT_ps[u % 2][:, :], copy).then_inc(hT_hi_ready, 1)

            take_gelu(0, 0)
            expert_rounds(act, step)
            for k in (UN - 2, UN - 1):
                weigh(NTILE - UN, k)

            for G in range(NG):
                act.wait_ge(out_ready, G + 1)
                act.dma_start(of[G * GQ:(G + 1) * GQ, :].rearrange("(t p) d -> p t d", p=P),
                              xs_[:, G * GT:(G + 1) * GT, :]).then_inc(stored, 16)
            act.wait_ge(stored, 16 * NG)

        @block.vector
        def _(dve):
            v = nc.vector
            links = [0]

            def link(ins):
                links[0] += 1
                ins.then_inc(vec, 1)
                dve.wait_ge(vec, links[0])

            v.memset(wo_aug[DH:DH + 1, D:D + 1], 1.0).then_inc(consts0, 1)
            v.memset(k_h1[DH:DH + 1, :].bitcast(f32), 1.0).then_inc(consts0, 1)

            dve.wait_ge(b_in, 32)
            for i in range(NB):
                v.tensor_copy(b_part[:, i], b_raw[:, :]).then_inc(bias_split, 1)
                dve.wait_ge(bias_split, 2 * i + 1)
                if i < NB - 1:
                    v.tensor_tensor(b_raw[:, :], b_raw[:, :], b_part[:, i], ALU.subtract).then_inc(bias_split, 1)
                    dve.wait_ge(bias_split, 2 * i + 2)

            def layernorm_stats(G, stats_of, mv_of, veps_of, ready):
                for t in range(GT):
                    ins = v.bn_stats(stats_of[:, t], xs_[:, G * GT + t])
                    if t < GT - 1:
                        ins.then_inc(vec, 1)
                        links[0] += 1
                link(ins)
                for t in range(GT):
                    ins = v.bn_aggr(mv_of[:, t], stats_of[:, t])
                    if t < GT - 1:
                        ins.then_inc(vec, 1)
                        links[0] += 1
                link(ins)
                v.tensor_scalar(veps_of[:, :], mv_of[:, :, 1], EPS, None, ALU.add).then_inc(ready, 1)

            def take_rest(s):
                G = max(k for k in range(NG) if FIRST_STEP[k] <= s)
                width = steps(G % GB)[s - FIRST_STEP[G]][2]
                dve.wait_ge(p_hi_ready, s + 1)
                wait_count(dve, pv_done, s - PR + 1)
                v.tensor_tensor(p_lo[:, s % PR, 0:width], prob[:, s % 2, 0:width],
                                p_hi[:, s % PR, 0:width].bitcast(f32), ALU.subtract).then_inc(p_lo_ready, 1)

            for stage, G, n in DVE_ORDER:
                r, cols, tiles = G % 2, slice(G * GQ, (G + 1) * GQ), slice(G * GT, (G + 1) * GT)
                if stage in READERS and "v" in READERS[stage]:
                    dve.wait_ge(bank_full, item(stage, G, n))
                    ps = bank(stage, G, n)
                if stage == "LN1":
                    dve.wait_ge(x_in[G], 16)
                    wait_count(dve, xn_ready, G)
                    wait_count(dve, rstd_ready, G)
                    layernorm_stats(G, stats, mv, veps, var_ready)
                elif stage == "NORM1":
                    dve.wait_ge(rstd_ready, G + 1)
                    if G >= 2:
                        dve.wait_ge(bank_full, item("XT", G - 2))
                    for t in range(GT):
                        ins = v.tensor_scalar(xn[:, r, t], xs_[:, G * GT + t], mv[:, t, 0:1], rstd[:, t:t + 1],
                                              ALU.subtract, ALU.mult)
                        if t < GT - 1:
                            ins.then_inc(vec, 1)
                            links[0] += 1
                    ins.then_inc(xn_ready, 1)
                elif stage == "QP":
                    dve.wait_ge(bank_act, ACT_READS[item(stage, G) - 1])
                    if G >= QR:
                        dve.wait_ge(scores_ready, FIRST_STEP[G - QR + 1])
                    v.tensor_tensor(q_lo[0:DH, G % QR], ps[0:DH, :], q_hi[0:DH, G % QR].bitcast(f32),
                                    ALU.subtract).then_inc(bank_dve, 1)
                elif stage == "KP":
                    dve.wait_ge(k_hi_ready, G + 1)
                    v.tensor_tensor(k_hl[DH:P, keys_of(G)], ps[DH:P, :], k_hl[DH:P, keys_of(G)].bitcast(f32),
                                    ALU.subtract).then_inc(bank_dve, 1)
                elif stage == "VP":
                    dve.wait_ge(bank_act, ACT_READS[item(stage, G) - 1])
                    v.tensor_tensor(V[:, values_of(G), 0:DH], ps[:, 0:GT * DH].rearrange("p (t d) -> p t d", t=GT),
                                    V[:, values_of(G), DH:2 * DH].bitcast(f32), ALU.subtract).then_inc(bank_dve, 1)
                elif stage == "AS":
                    if FIRST_STEP[G] + n > 0:
                        take_rest(FIRST_STEP[G] + n - 1)
                    if FIRST_STEP[G] + n == FIRST_STEP[NG] - 1:
                        take_rest(FIRST_STEP[NG] - 1)
                elif stage == "MX":
                    t, c = n
                    g = G % GB
                    if n == (0, 0):
                        wait_count(dve, mneg_ready, G)
                    width = GQ if c < g else (t + 1) * P
                    v.tensor_reduce(mpart[:, t, c:c + 1], ps[:, 0:width], AX.X, ALU.max).then_inc(bank_dve, 1)
                elif stage == "MR":
                    g = G % GB
                    dve.wait_ge(bank_dve, DVE_READS[item("MX", G, (GT - 1, g)) - 1])
                    if G >= 1:
                        dve.wait_ge(bank_full, item("MR", G - 1))
                    else:
                        dve.wait_ge(consts0, N_FILLS)
                    v.tensor_reduce(mneg[:, :, DH], mpart[:, :, 0:g + 1], AX.X, ALU.max,
                                    negate=True).then_inc(mneg_ready, 1)
                elif stage == "OP":
                    both_tiles = ps[:, 0:2 * (D + 1)].rearrange("p (t d) -> p t d", t=2)
                    if G or n:
                        dve.wait_ge(bank_dve, DVE_READS[item("OP", *((G, 0) if n else (G - 1, 1))) - 1])
                    link(v.reciprocal(rsum[:, :], both_tiles[:, :, D]))
                    for t in range(2):
                        tile = G * GT + 2 * n + t
                        if t == 0 and n == 0:
                            dve.wait_ge(xn_ready, G + 1)
                        ins = v.scalar_tensor_tensor(xs_[:, tile], both_tiles[:, t, 0:D], rsum[:, t:t + 1],
                                                     xs_[:, tile], ALU.mult, ALU.add)
                        if t == 0:
                            ins.then_inc(x2_ready, 1)
                    ins.then_inc(bank_dve, 1)
                elif stage == "LN2":
                    dve.wait_ge(bank_dve, DVE_READS[item("OP", G, 1) - 1])
                    dve.wait_ge(x2_ready, 2 * G + 2)
                    wait_count(dve, x2n_ready, G)
                    wait_count(dve, rstd2_ready, G)
                    layernorm_stats(G, stats, mv2, veps2, var2_ready)
                elif stage == "NORM2":
                    dve.wait_ge(rstd2_ready, G + 1)
                    if G >= 2:
                        dve.wait_ge(sent[r], 16 * TOP * GT * (G // 2))
                    for t in range(GT):
                        ins = v.tensor_scalar(rows[:, r, t, 0, 0:D], xs_[:, G * GT + t], mv2[:, t, 0:1],
                                              rstd2[:, t:t + 1], ALU.subtract, ALU.mult)
                        if t < GT - 1:
                            ins.then_inc(vec, 1)
                            links[0] += 1
                    ins.then_inc(x2n_ready, 1)
                elif stage == "LG":
                    wait_count(dve, slots_ready, G)
                    v.tensor_copy(lg[:, :, :], ps[:, 0:GT * E].rearrange("p (t e) -> p t e", t=GT)).then_inc(bank_dve, 1)
                    dve.wait_ge(bank_dve, DVE_READS[item("LG", G) - 1])
                    for t in range(GT):
                        v.max(top8[:, t], lg[:, t]).then_inc(vec, 1)
                    for t in range(GT):
                        dve.wait_ge(vec, links[0] + t + 1)
                        ins = v.max_index(top_i[:, t], top8[:, t], lg[:, t])
                        if t < GT - 1:
                            ins.then_inc(vec, 1)
                    links[0] += 2 * GT - 1
                    link(ins)
                    wait_count(dve, egap_ready, G)
                    v.tensor_tensor(gap[:, :], top8[:, :, 1], top8[:, :, 0], ALU.subtract).then_inc(gap_ready, 1)
                    link(v.tensor_copy(top_f[:, :, :], top_i[:, :, 0:TOP]))
                    for k in range(TOP):
                        link(v.tensor_tensor(pick[:, k], expert_id[:, :].unsqueeze(1).to_broadcast((P, GT, E)),
                                             top_f[:, :, k:k + 1].to_broadcast((P, GT, E)), ALU.is_equal))
                    v.tensor_tensor(both[:, :, :], pick[:, 0], pick[:, 1], ALU.add).then_inc(picks_ready, 1)
                elif stage == "RT":
                    dve.wait_ge(egap_ready, G + 1)
                    dve.wait_ge(x2n_ready, G + 1)
                    v.tensor_copy(rows[:, r, :, 1, 0:D], rows[:, r, :, 0, 0:D]).then_inc(vec, 1)
                    links[0] += 1
                    link(v.tensor_scalar(veps2[:, :], egap[:, :], 1.0, None, ALU.add))
                    link(v.reciprocal(rows[:, r, :, 0, D], veps2[:, :]))
                    link(v.tensor_tensor(rows[:, r, :, 1, D], egap[:, :], rows[:, r, :, 0, D], ALU.mult))
                    link(v.tensor_copy(rows[:, r, :, :, D + 1].bitcast(i32), dest[:, tiles, :]))
                elif stage == "RK":
                    link(v.tensor_copy(rank[:, :, :], ps[:, 0:GT * E].rearrange("p (t e) -> p t e", t=GT)))
                    for k in range(TOP):
                        link(v.tensor_tensor(ranked[:, k], pick[:, k], rank[:, :, :], ALU.mult))
                    link(v.tensor_reduce(slot_f[:, :, :], ranked[:, :, :, :], AX.X, ALU.add))
                    v.scalar_tensor_tensor(slot[:, r], top_f[:, :, :].rearrange("p t k -> p k t"), float(REGION),
                                           slot_f[:, :, :], ALU.mult, ALU.add).then_inc(slots_ready, 1)
                    link(v.tensor_reduce(bothsum[:, :], both[:, :, :].rearrange("p t e -> p e t"), AX.X, ALU.add))
                    link(v.tensor_tensor(seen[:, :], seen[:, :], bothsum[:, :], ALU.add))
                    v.tensor_copy(seen_b[:, :], seen[:, :]).then_inc(bank_dve, 1)
                elif stage == "CN":
                    link(v.tensor_copy(cnt[:, :], ps[:, 0:E]))
                    v.scalar_tensor_tensor(pad_at[:, :], expert_id[:, :], float(REGION), cnt[:, :],
                                           ALU.mult, ALU.add).then_inc(pad_at_ready, 1)
                    link(v.tensor_scalar(cnt_i[:, :], cnt[:, :], float(P - 1), None, ALU.add))
                    link(v.tensor_scalar(nt_i[:, :], cnt_i[:, :], P.bit_length() - 1, None, ALU.logical_shift_right))
                    link(v.tensor_copy(nt_f[:, :], nt_i[:, :]))
                    link(v.tensor_tensor(cum8[:, :, :], incl[:, :, :],
                                         nt_f[:, :].unsqueeze(1).to_broadcast((P, E, E)), ALU.mult))
                    link(v.tensor_reduce(cend[:, :], cum8[:, :, :], AX.X, ALU.add))
                    link(v.tensor_scalar(skip[:, :], nt_f[:, :], -float(P), float(REGION), ALU.mult, ALU.add))
                    link(v.tensor_tensor(past[:, :, :], tile_no[:, :].unsqueeze(2).to_broadcast((P, NTILE, E)),
                                         cend[:, :].unsqueeze(1).to_broadcast((P, NTILE, E)), ALU.is_ge))
                    link(v.tensor_reduce(te_f[:, :], past[:, :, :], AX.X, ALU.add))
                    link(v.tensor_scalar(tile_expert[:, :], te_f[:, :], float(E - 1), None, ALU.min))
                    link(v.tensor_tensor(past2[:, :, :], past[:, :, :],
                                         skip[:, :].unsqueeze(1).to_broadcast((P, NTILE, E)), ALU.mult))
                    link(v.tensor_reduce(tr_f[:, :], past2[:, :, :], AX.X, ALU.add))
                    link(v.scalar_tensor_tensor(te_f[:, :], tile_no[:, :], float(P), tr_f[:, :], ALU.mult, ALU.add))
                    v.tensor_scalar(tile_row[:, :], te_f[:, :], float(E * REGION), None,
                                    ALU.min).then_inc(table_ready, 1)

            def take_rows(base, k):
                dve.wait_ge(xgT_full, base + k + 1)
                wait_count(dve, h_full, base + (k + 1 - XR))
                ps = wk[k % 2][:, 0:P]
                v.tensor_copy(xgT_hi[:, k % XR], ps).then_inc(xgT_hi_ready, 1)
                wait_count(dve, y_sent[k % UN], (16 // UN) * base + 16 * (k // UN))
                v.tensor_copy(meta[:, k % UN], xg[:, k % UN, D:ROW]).then_inc(meta_ready, 1)
                dve.wait_ge(xgT_hi_ready, base + k + 1)
                v.tensor_tensor(xgT_lo[:, k % XR], ps, xgT_hi[:, k % XR].bitcast(f32),
                                ALU.subtract).then_inc(xgT_ready, 1)

            def weigh(base, k):
                dve.wait_ge(y_rest_ready, base + k + 1)
                v.scalar_tensor_tensor(y[:, k % UN], pv[k % 2][:, 0:D], meta[:, k % UN, 0:1], y[:, k % UN],
                                       ALU.mult, ALU.add).then_inc(y_ready, 1)

            def step(base, u, has):
                if has(3):
                    take_rows(base, u + 3)
                if has(-2):
                    weigh(base, u - 2)
                dve.wait_ge(hT_hi_ready, base + u + 1)
                wait_count(dve, y_full, base + (u + 1 - XR))
                v.tensor_tensor(hT_lo[:, u % XR], hT_ps[u % 2][:, :],
                                hT_hi[:, u % XR].bitcast(f32), ALU.subtract).then_inc(hT_ready, 1)

            for k in range(3):
                take_rows(0, k)
            expert_rounds(dve, step)
            for k in (UN - 2, UN - 1):
                weigh(NTILE - UN, k)

            for G in range(NG):
                results, tiles = yg[G % len(yg)], slice(G * GT, (G + 1) * GT)
                dve.wait_ge(yg_in[G], 16)
                link(v.tensor_tensor(xs_[:, tiles], xs_[:, tiles], results[:, :, 0:D], ALU.add))
                v.tensor_tensor(xs_[:, tiles], xs_[:, tiles], results[:, :, D:2 * D], ALU.add).then_inc(out_ready, 1)

        @block.tensor
        def _(pe):
            t_ = nc.tensor

            def free_bank(stage, G, n):
                k = ITEM[(stage, G, n)]
                if k >= BR:
                    wait_count(pe, bank_act, ACT_READS[k - BR])
                    wait_count(pe, bank_dve, DVE_READS[k - BR])
                return bank(stage, G, n)

            pe.wait_ge(wqkv_in, 112)
            pe.wait_ge(consts, N_CONSTS)
            t_.transpose(st[0][:, 0:P], wq_dup[:, :], ident[:, :])
            t_.transpose(st[0][:, P:2 * P], wk_dup[:, :], ident[:, :])
            t_.transpose(st[0][:, 2 * P:2 * P + DH], wv_[:, :], ident[0:DH, 0:DH])
            t_.transpose(st[0][:, 3 * P:4 * P], wo2[:, :], ident[:, :]).then_inc(wT_ready, 1)

            def product_with_v(s):
                G = max(k for k in range(NG) if FIRST_STEP[k] <= s)
                n = s - FIRST_STEP[G]
                blocks = steps(G % GB)
                pe.wait_ge(p_lo_ready, s + 1)
                if n == 0:
                    wait_count(pe, oT_ready, 2 * G)
                kb, q0, w = blocks[n]
                first, last = n == 0, n == len(blocks) - 1
                vt = values_at(G, kb)
                hi, lo = p_hi[:, s % PR, 0:w], p_lo[:, s % PR, 0:w]
                t_.matmul(pv[0][:, q0:q0 + w], V[:, vt, 0:2 * DH], hi, start=first, stop=last)
                t_.matmul(pv[1][0:DH + 1, q0:q0 + w], V[:, vt, DH:2 * DH + 1], lo, start=first, stop=False)
                ins = t_.matmul(pv[1][0:DH + 1, q0:q0 + w], sum_col[:, :], hi, start=False, stop=last)
                ins.then_inc(pv_done, 1)

            for stage, G, n in SCHEDULE:
                r, b, g = G % 2, G // GB, G % GB
                if stage in READERS:
                    ps = free_bank(stage, G, n)
                if stage == "XT":
                    pe.wait_ge(xn_ready, G + 1)
                    for t in range(GT):
                        ins = t_.transpose(ps[:, t * P:(t + 1) * P], xn[:, r, t], ident[:, :])
                    ins.then_inc(bank_full, 1)
                elif stage in ("QP", "KP"):
                    if stage == "QP":
                        pe.wait_ge(wT_copied, 5)
                        pe.wait_ge(bank_act, ACT_READS[item("XT", G) - 1])
                    t_.matmul(ps[:, :], (wqT if stage == "QP" else wkT)[:, :], xT[:, r], start=True,
                              stop=True).then_inc(bank_full, 1)
                elif stage == "VP":
                    for t in range(GT):
                        ins = t_.matmul(ps[:, t * DH:(t + 1) * DH], xT[:, r, t * P:(t + 1) * P], wvT[:, :],
                                        start=True, stop=True)
                    ins.then_inc(bank_full, 1)
                elif stage == "MX":
                    t, c = n
                    width = GQ if c < g else (t + 1) * P
                    k0 = keys_of(b * GB + c).start
                    if n == (0, 0):
                        pe.wait_ge(bank_act, ACT_READS[item("QP", G) - 1])
                        pe.wait_ge(bank_dve, DVE_READS[item("KP", G) - 1])
                    ins = t_.matmul(ps[:, 0:width], q_hi[:, G % QR, t * P:(t + 1) * P], k_hl[:, k0:k0 + width],
                                    start=True, stop=(c < g))
                    if c == g:
                        ins = t_.matmul(ps[:, width - P:width], ident_b[:, :], mask_qk[:, :], start=False, stop=True)
                    ins.then_inc(bank_full, 1)
                elif stage == "MR":
                    pe.wait_ge(mneg_ready, G + 1)
                    for t in range(GT):
                        ins = t_.matmul(ps[0:DH + 1, t * P:(t + 1) * P], mneg[:, t, 0:DH + 1], ident_r[:, :],
                                        start=True, stop=True)
                    ins.then_inc(bank_full, 1)
                elif stage == "AS":
                    s = FIRST_STEP[G] + n
                    if n == 0:
                        pe.wait_ge(bank_act, ACT_READS[item("MR", G) - 1])
                        pe.wait_ge(bank_dve, DVE_READS[item("QP", G) - 1])
                    wait_count(pe, p_hi_ready, s - BR + 1)
                    kb, q0, w = steps(g)[n]
                    k0 = keys_of(b * GB + kb // GT).start + kb % GT * P
                    diagonal = kb >= GT * g
                    o = st[s % BR]
                    t_.matmul(o[:, 0:w], k_hl[:, k0:k0 + P], q_hi[:, G % QR, q0:q0 + w], start=True, stop=False)
                    ins = t_.matmul(o[:, 0:w], k_h1[:, k0:k0 + P], q_lo[:, G % QR, q0:q0 + w],
                                    start=False, stop=not diagonal)
                    if diagonal:
                        ins = t_.matmul(o[:, 0:P], ident_b[:, :], mask_kq[:, :], start=False, stop=True)
                    ins.then_inc(scores_ready, 1)
                    if s >= LAG:
                        product_with_v(s - LAG)
                elif stage == "AE":
                    product_with_v(FIRST_STEP[NG] - LAG + n)
                elif stage == "OP":
                    pe.wait_ge(oT_ready, 2 * (G + 1))
                    pe.wait_ge(wout_in, 16)
                    for t in range(2):
                        q0 = (2 * n + t) * P
                        o = ps[:, t * (D + 1):(t + 1) * (D + 1)]
                        t_.matmul(o, oA[:, q0:q0 + P], wo_dup[:, :], start=True, stop=False)
                        ins = t_.matmul(o, oB[:, q0:q0 + P], wo_aug[:, :], start=False, stop=True)
                    ins.then_inc(bank_full, 1)
                elif stage == "X2T":
                    pe.wait_ge(x2n_ready, G + 1)
                    for t in range(GT):
                        ins = t_.transpose(ps[:, t * P:(t + 1) * P], rows[:, r, t, 0, 0:D], ident[:, :])
                    ins.then_inc(bank_full, 1)
                elif stage == "LG":
                    pe.wait_ge(gate_in, 16)
                    pe.wait_ge(bank_act, ACT_READS[item("X2T", G) - 1])
                    for t in range(GT):
                        ins = t_.matmul(ps[:, t * E:(t + 1) * E], x2T[:, t * P:(t + 1) * P], gate[:, :],
                                        start=True, stop=True)
                    ins.then_inc(bank_full, 1)
                elif stage == "RK":
                    pe.wait_ge(picks_ready, G + 1)
                    if G >= 1:
                        pe.wait_ge(bank_dve, DVE_READS[item("RK", G - 1) - 1])
                    for t in range(GT):
                        o = ps[:, t * E:(t + 1) * E]
                        t_.matmul(o, ones_b[:, :], seen_b[:, :], start=True, stop=False)
                        for t2 in range(t):
                            t_.matmul(o, ones_b[:, :], both[:, t2], start=False, stop=False)
                        ins = t_.matmul(o, tri[:, :], both[:, t], start=False, stop=True)
                    ins.then_inc(bank_full, 1)
                elif stage == "CN":
                    pe.wait_ge(bank_dve, DVE_READS[item("RK", NG - 1) - 1])
                    t_.matmul(ps[:, 0:E], ones_b[:, :], seen_b[:, :], start=True, stop=True).then_inc(bank_full, 1)

            def transpose_rows(base, k):
                pe.wait_ge(xg_in[k % UN], (16 // UN) * base + 16 * (k // UN + 1))
                wait_count(pe, xgT_ready, base + (k - 1))
                t_.transpose(wk[k % 2][:, 0:P], xg[:, k % UN, 0:D], ident[:, :]).then_inc(xgT_full, 1)

            experts = {}

            def expert(base, k):
                if k < 0:
                    return pe.value_load(tile_expert[0:1, bass.ds(base + k, 1)], min_val=0, max_val=E - 1)
                if (str(base), k) not in experts:
                    experts[(str(base), k)] = pe.value_load(tile_expert[0:1, bass.ds(base + k, 1)], min_val=0,
                                                            max_val=E - 1)
                return experts[(str(base), k)]

            def first_product(base, k):
                e = expert(base, k)
                pe.wait_ge(xgT_ready, base + k + 1)
                wait_count(pe, h_ready, base + (k - 1))
                o = h_ps[k % 2][:, :]
                hi, lo = xgT_hi[:, k % XR], xgT_lo[:, k % XR]
                w_hi, w_lo = (w1p[:, bass.ds(e, 1), i].rearrange("p a f -> p (a f)") for i in range(2))
                t_.matmul(o, hi, w_hi, start=True, stop=False)
                t_.matmul(o, hi, w_lo, start=False, stop=False)
                t_.matmul(o, lo, w_hi, start=False, stop=False)
                t_.matmul(o, ones_b[0:NB, :], b1_r[:, bass.ds(e * F, F)], start=False, stop=True).then_inc(h_full, 1)

            def second_product(base, k):
                e = expert(base, k)
                pe.wait_ge(hT_ready, base + k + 1)
                wait_count(pe, y_ready, base + (k - 1))
                for c in range(FC):
                    hi, lo = (t[:, k % XR, c * P:(c + 1) * P] for t in (hT_hi, hT_lo))
                    w = w2p[:, bass.ds(e, 1), c]
                    t_.matmul(pv[k % 2][:, 0:2 * D], hi, w.rearrange("p a i d -> p (a i d)"), start=(c == 0), stop=False)
                    t_.matmul(pv[k % 2][:, 0:D], lo, w[:, :, 0].rearrange("p a d -> p (a d)"), start=False, stop=False)
                t_.matmul(pv[k % 2][:, 0:D], ones_b[0:NB, :], b2_r[:, bass.ds(e * D, D)], start=False,
                          stop=True).then_inc(y_full, 1)

            def step(base, u, has):
                if has(1):
                    first_product(base, u + 1)
                if has(3):
                    transpose_rows(base, u + 3)
                if has(-2):
                    second_product(base, u - 2)
                pe.wait_ge(h_ready, base + u + 1)
                wait_count(pe, hT_ready, base + (u - 1))
                for c in range(FC):
                    ins = t_.transpose(hT_ps[u % 2][:, c * P:(c + 1) * P], h[:, u % 2, c * P:(c + 1) * P], ident[:, :])
                ins.then_inc(hT_full, 1)

            pe.wait_ge(table_ready, 1)
            pe.wait_ge(w_lo_ready, 2 * E)
            pe.wait_ge(bias_in, 32 * NB)
            for k in range(3):
                transpose_rows(0, k)
            first_product(0, 0)
            expert_rounds(pe, step)
            for k in (UN - 2, UN - 1):
                second_product(NTILE - UN, k)


_INS = ['L0_attn_x', 'L0_attn_w_qkv', 'L0_attn_w_out', 'L0_attn_b_out', 'L0_ffn_gate_w',
        'L0_ffn_w1', 'L0_ffn_b1', 'L0_ffn_w2', 'L0_ffn_b2']
_OUTS = [((2, 2048, 128), 'float32')]


def kernel(**inputs):
    import numpy as _np
    import concourse.bacc as _bacc
    from concourse import mybir as _mybir
    from concourse.bass_utils import run_bass_kernel_spmd as _run

    nc = _bacc.Bacc("TRN2", target_bir_lowering=False, num_devices=1)
    arrays, args = {}, []
    for name in _INS:
        a = _np.ascontiguousarray(inputs[name])
        arrays[f"in_{name}_dram"] = a
        args.append(nc.dram_tensor(f"in_{name}_dram", a.shape, _mybir.dt.from_np(a.dtype), kind="ExternalInput").ap())
    for i, (shape, dtype) in enumerate(_OUTS):
        dt = _mybir.dt.from_np(_np.dtype(dtype))
        args.append(nc.dram_tensor(f"out_{i}_dram", shape, dt, kind="ExternalOutput").ap())
    preln_attention_moe(nc, *args)
    r = _run(nc, [arrays], core_ids=[0])
    return r.results[0]["out_0_dram"]
```

```python
import concourse.bass as bass
from concourse import mybir
from contextlib import ExitStack


def preln_attention_moe(nc, x, w_qkv, w_out, b_out, gate_w, w1, b1, w2, b2, out):
    f32, f32r, bf16 = mybir.dt.float32, mybir.dt.float32r, mybir.dt.bfloat16
    i32, u32 = mybir.dt.int32, mybir.dt.uint32
    ALU, ACT, AX = mybir.AluOpType, mybir.ActivationFunctionType, mybir.AxisListType

    P = 128
    B, S, D = x.shape
    DH = w_out.shape[1]
    E, _, F = w1.shape
    TOP = 2
    T = B * S
    NT = T // P
    GT = 4
    GQ = GT * P
    NG = NT // GT
    GB = S // GQ
    FC = F // P
    SCALE = float(DH) ** -0.5
    EPS = 1e-5
    NEG = -1e38
    REGION = T + P
    ROW = D + 2
    NSLOT = T * TOP
    MAXT = NSLOT // P + E - 1
    UN = 8
    PE_UN = 2 * UN
    KR, VR = 6, 6
    QR = 3
    LAG = 3
    PB = 3
    PR, BR = LAG + 1, 3
    ROUNDS = -(-MAXT // UN)
    LAST = MAXT - (ROUNDS - 1) * UN
    FAR = 1 << 20

    N_FILLS, N_CONSTS = 21, 10

    xf = x.rearrange("b n d -> (b n) d")
    of = out.rearrange("b n d -> (b n) d")
    disp = nc.dram_tensor("dispatched_rows", (E * REGION + P, ROW), f32, kind="Internal").ap()
    ys = nc.dram_tensor("expert_results", (NSLOT, D), f32, kind="Internal").ap()

    def steps(g):
        return [(kb, max(0, kb - GT * g) * P, GQ - max(0, kb - GT * g) * P) for kb in range(GT * (g + 1))]

    FIRST_STEP = [0]
    for G in range(NG):
        FIRST_STEP.append(FIRST_STEP[-1] + len(steps(G % GB)))

    def rest_on_pool(s):
        return s % 4 == 3

    def rests(s, on_pool):
        return sum(rest_on_pool(k) == on_pool for k in range(s + 1))

    READERS = {"XT": "a", "QP": "av", "KP": "av", "VP": "av", "MX": "v", "MR": "a",
               "OP": "v", "X2T": "a", "LG": "v", "RK": "v", "CN": "v"}

    PACE, XT_GAP, MX_GAP, LN1_LEAD, NORM1_GAP, MR_GAP, AS_GAP, OE_EARLY = 0.58, 0.0, 0.0, 8.09, 1.06, 1.0, 0.62, 0.5
    BACK = (("OP", 0), ("OP", 1), ("LN2", 0), ("NORM2", 0), ("X2T", 0), ("LG", 0), ("RT", 0), ("RK", 0))
    BACK_GAPS, SC_GAP, SC_PACE = (0.85, 0.88, 0.97, 1.0, 1.87, 1.56, 1.0, 1.95), 0.75, 1.42
    EARLIEST, WS_AT = -1.2, 1.4
    ACT_LATE = {"XT": 0.2, "QP": 0.04, "KP": 0.21, "VP": 0.2, "MR": 0.04, "X2T": 0.2, "RT": 0.25, "WS": 0.19}
    DVE_LATE = {"QP": 0.2, "KP": 0.64, "VP": 0.38, "MX": 0.35, "MR": 0.32, "OP": 0.32, "LG": 0.32, "RT": 0.27,
                "RK": 0.32, "LN1": 0.32, "NORM1": 0.32, "LN2": 0.1, "NORM2": 0.32, "CN": 0.32}
    timed = [(s, 0, ("AS", G, s - FIRST_STEP[G])) for G in range(NG) for s in range(FIRST_STEP[G], FIRST_STEP[G + 1])]
    timed += [(FIRST_STEP[NG] + n, 0, ("AE", NG - 1, n)) for n in range(LAG)]
    start, xt_at = FIRST_STEP[NG], {}
    for G in reversed(range(NG)):
        parts = [("MX", (t, c)) for t in range(GT) for c in range(G % GB + 1)]
        last = min(start, FIRST_STEP[G] - AS_GAP - MR_GAP)
        timed.append((last + MR_GAP, 1, ("MR", G, 0)))
        gaps = [0, XT_GAP + PACE, PACE, PACE, PACE + MX_GAP] + [PACE] * (len(parts) - 1)
        parts = [("XT", 0), ("QP", 0), ("KP", 0), ("VP", 0)] + parts
        start = max(last - sum(gaps) - PACE, -2.0 if G == 0 else EARLIEST)
        squeeze = (last - start) / (sum(gaps) + PACE)
        timed += [(start + squeeze * sum(gaps[:i + 1]), 1, (part, G, n)) for i, (part, n) in enumerate(parts)]
        xt_at[G] = start
    norm = -9
    for G in range(NG):
        ln = max(xt_at[G] - LN1_LEAD, norm + 0.1)
        norm = max(ln + NORM1_GAP, xt_at[G - 2] + 0.5 if G >= 2 else norm)
        timed += [(ln, 1, ("LN1", G, 0)), (norm, 1, ("NORM1", G, 0))]
    end = 0
    for G in range(NG):
        begin = FIRST_STEP[G + 1] + LAG - OE_EARLY
        timed.append((begin, 2, ("OE", G, 0)))
        end = max(end, begin)
        for (part, n), gap_before in zip(BACK, BACK_GAPS):
            end += gap_before
            timed.append((end, 2, (part, G, n)))
        timed += [(end + SC_GAP + SC_PACE * t, 2, ("SC", G, t)) for t in range(GT)]
        timed.append((FIRST_STEP[G] + WS_AT, 3, ("WS", G, 0)))
    timed += [(end + 1, 3, ("CN", NG - 1, 0)), (FIRST_STEP[1], 3, ("BIAS", 0, 0))]

    def order(late):
        res, bank_time = [], -99
        for t, k, part in sorted(timed, key=lambda t: t[:2]):
            at = t + late.get(part[0], 0)
            if part[0] in READERS:
                at = bank_time = max(at, bank_time)
            res.append((at, k, len(res), part))
        return [part for _, _, _, part in sorted(res)]

    SCHEDULE, ACT_ORDER, DVE_ORDER = order({}), order(ACT_LATE), order(DVE_LATE)

    ITEM, ACT_READS, DVE_READS = {}, [], []
    for part in SCHEDULE:
        if part[0] in READERS:
            who = READERS[part[0]]
            ITEM[part] = len(ITEM)
            ACT_READS.append((ACT_READS[-1] if ACT_READS else 0) + ("a" in who))
            DVE_READS.append((DVE_READS[-1] if DVE_READS else 0) + ("v" in who))

    ctx = ExitStack()
    with ctx:
        def sb(name, shape, dt=f32):
            return ctx.enter_context(nc.sbuf_tensor(name, shape, dt))

        def pb(name, shape, dt=f32):
            return ctx.enter_context(nc.psum_tensor(name, shape, dt))

        def sem(name):
            return ctx.enter_context(nc.semaphore(name))

        ident = sb("ident", [P, P])
        ident_r = sb("ident_r", [P, P], f32r)
        ident_b = sb("ident_b", [P, P], bf16)
        mask_kq = sb("mask_kq", [P, P], bf16)
        mask_qk = sb("mask_qk", [P, P], bf16)
        tri = sb("tri", [P, P], bf16)
        ones_b = sb("ones_b", [P, P], bf16)
        sum_col = sb("sum_col", [P, DH + 1], f32r)
        mhalf = sb("mhalf", [P, GT])
        expert_id = sb("expert_id", [P, E])
        token_i = sb("token_i", [P, TOP, NT], i32)
        token_no = sb("token_no", [P, TOP, NT])
        second = sb("second", [P, GT])
        tile_no_i = sb("tile_no_i", [P, MAXT], i32)
        expert_i = sb("expert_i", [P, E], i32)
        tile_no = sb("tile_no", [P, MAXT])
        incl = sb("incl", [P, E, E])
        wq_dup, wk_dup, wv_ = sb("wq_dup", [P, D]), sb("wk_dup", [P, D]), sb("wv_", [DH, D])
        wo2 = sb("wo2", [P, 2 * DH])
        wqT, wkT, wvT = sb("wqT", [D, P]), sb("wkT", [D, P]), sb("wvT", [D, DH])
        wo_dup = sb("wo_dup", [P, D + 1])
        wo_aug = sb("wo_aug", [DH + 1, D + 1])
        gate = sb("gate", [D, E])
        w_raw = sb("w_raw", [P, 2, F])
        w1p = sb("w1p", [P, E, 2, F], f32r)
        w2p = sb("w2p", [P, E, FC, 2, D], f32r)
        NB, NB1, NB2 = 3, E * F // P, E * D // P
        b_raw = sb("b_raw", [P, NB1 + NB2])
        b_part = sb("b_part", [P, NB, NB1 + NB2], bf16)
        b1_r = sb("b1_r", [NB, E * F], bf16)
        b2_r = sb("b2_r", [NB, E * D], bf16)
        xs_ = sb("xs_", [P, NT, D])
        stats = sb("stats", [P, GT, 6])
        mv = sb("mv", [P, GT, 2])
        veps = sb("veps", [P, GT])
        rstd = sb("rstd", [P, GT])
        mv2 = sb("mv2", [P, GT, 2])
        veps2 = sb("veps2", [P, GT])
        rstd2 = sb("rstd2", [P, GT])
        xn2 = sb("xn", [P, 2, GT * D])
        xn = xn2[:, :, :].rearrange("p r (t d) -> p r t d", t=GT)
        xT = sb("xT", [D, 2, GQ])
        q_hi = sb("q_hi", [P, QR, GQ], f32r)
        q_lo = sb("q_lo", [DH + 1, QR, GQ], f32r)
        k_hl = sb("k_hl", [P, KR * GQ], f32r)
        k_h1 = sb("k_h1", [DH + 1, KR * GQ], f32r)
        V = sb("V", [P, VR * GT, 2 * DH + 2], f32r)
        mpart = sb("mpart", [P, GT, GB])
        mneg = sb("mneg", [P, GT, DH + 2], f32r)
        prob = sb("prob", [P, PB, GQ])
        p_hi = sb("p_hi", [P, PR, GQ], f32r)
        p_lo = sb("p_lo", [P, PR, GQ], f32r)
        oA = sb("oA", [P, GQ])
        oB = sb("oB", [DH + 1, GQ])
        rsum = sb("rsum", [P, 2])
        rows = sb("rows", [P, 2, GT, TOP, ROW])
        x2T = sb("x2T", [D, GQ])
        top8 = sb("top8", [P, GT, 8])
        top_i = sb("top_i", [P, GT, 8], u32)
        top_f = sb("top_f", [P, GT, TOP])
        pick = sb("pick", [P, TOP, GT, E])
        both = sb("both", [P, 2, 1 + GT, E], bf16)
        gap = sb("gap", [P, GT])
        egap = sb("egap", [P, GT])
        ranked = sb("ranked", [P, TOP, GT, E])
        slot_f = sb("slot_f", [P, TOP, GT])
        slot = sb("slot", [P, 2, TOP, GT], u32)
        cnt = sb("cnt", [P, E])
        cnt_i = sb("cnt_i", [P, E], i32)
        pad_at = sb("pad_at", [P, E], i32)
        nt_i = sb("nt_i", [P, E], i32)
        nt_f = sb("nt_f", [P, E])
        cum8 = sb("cum8", [P, E, E])
        cend = sb("cend", [P, E])
        skip = sb("skip", [P, E])
        past = sb("past", [P, MAXT, E])
        past2 = sb("past2", [P, MAXT, E])
        te_f = sb("te_f", [P, MAXT])
        tr_f = sb("tr_f", [P, MAXT])
        tile_expert = sb("tile_expert", [P, MAXT], i32)
        tile_row = sb("tile_row", [P, MAXT], i32)
        pad_rows = sb("pad_rows", [P, ROW])
        lane_f = sb("lane_f", [P, UN])
        lane_i = sb("lane_i", [P, UN], i32)
        lane_wait = sb("lane_wait", [P, UN], i32)
        weight = sb("weight", [P, UN])
        goes_to = sb("goes_to", [P, UN], u32)
        XR = 4
        xg = rows[:, 0].rearrange("p t k n -> p (t k) n")
        xgT_hi, xgT_lo = (q_hi[:, i].rearrange("p (i n) -> p i n", i=XR) for i in range(2))
        h = prob[:, 0:2]
        y = w_raw[:, :, :].rearrange("p a (i d) -> p (a i) d", d=D)
        hT_hi = k_hl[:, 0:XR * F].rearrange("p (i f) -> p i f", i=XR)
        hT_lo = p_hi[:, 0:XR]
        halves = [b[:, :].rearrange("p a n -> p (a n)")[:, i * GT * D:(i + 1) * GT * D]
                  for b in (xn2, xT, rows[:, 1].rearrange("p t k n -> p t (k n)"),
                            prob, w_raw, rows[:, 0].rearrange("p t k n -> p t (k n)")) for i in range(2)]
        halves = halves[0:6] + [oA[:, :], x2T[:, :]] + halves[6:]
        halves = [b.rearrange("p (t d) -> p t d", t=GT) for b in halves]
        lower, higher = halves[0:NG], halves[NG:] + halves[0:2]

        st = [pb(f"st{i}", [P, GQ]) for i in range(BR)]
        pv = [pb(f"pv{i}", [P, GQ]) for i in range(2)]
        wk = [pb(f"wk{i}", [P, GQ]) for i in range(BR)]
        h_ps, hT_ps = st[0:2], (st[2], wk[2])

        x_in = [sem(f"x_in{G}") for G in range(NG)]
        wqkv_in, wout_in, gate_in, w12_in = sem("wqkv_in"), sem("wout_in"), sem("gate_in"), sem("w12_in")
        w_hi_ready, w_lo_ready = sem("w_hi_ready"), sem("w_lo_ready")
        b_in, bias_split, bias_in = sem("b_in"), sem("bias_split"), sem("bias_in")
        consts0, consts = sem("consts0"), sem("consts")
        wT_ready, wT_copied = sem("wT_ready"), sem("wT_copied")
        vec = sem("vec")
        var_ready, rstd_ready = sem("var_ready"), sem("rstd_ready")
        xn_ready = sem("xn_ready")
        k_hi_ready = sem("k_hi_ready")
        mneg_ready = sem("mneg_ready")
        bank_full, bank_act, bank_dve = sem("bank_full"), sem("bank_act"), sem("bank_dve")
        scores_ready, probs_ready, pv_done = sem("scores_ready"), sem("probs_ready"), sem("pv_done")
        p_hi_ready, p_lo_ready, p_lo_pool_ready = sem("p_hi_ready"), sem("p_lo_ready"), sem("p_lo_pool_ready")
        o_ready, x2_ready = sem("o_ready"), sem("x2_ready")
        var2_ready, rstd2_ready = sem("var2_ready"), sem("rstd2_ready")
        x2n_ready = sem("x2n_ready")
        gap_ready, egap_ready, picks_ready = sem("gap_ready"), sem("egap_ready"), sem("picks_ready")
        slots_ready, seen_ready = sem("slots_ready"), sem("seen_ready")
        copies_ready = sem("copies_ready")
        sent = [sem(f"sent{i}") for i in range(2)]
        pad_at_ready, table_ready, padded = sem("pad_at_ready"), sem("table_ready"), sem("padded")
        xg_in = [sem(f"xg_in{u}") for u in range(UN)]
        xgT_full, xgT_hi_ready, xgT_ready = sem("xgT_full"), sem("xgT_hi_ready"), sem("xgT_ready")
        meta_ready, hT_hi_ready = sem("meta_ready"), sem("hT_hi_ready")
        h_full, h_ready = sem("h_full"), sem("h_ready")
        hT_full, hT_ready = sem("hT_full"), sem("hT_ready")
        y_full, y_ready = sem("y_full"), sem("y_ready")
        y_rest_ready = sem("y_rest_ready")
        lanes_ready = sem("lanes_ready")
        scatters_begun = sem("scatters_begun")
        y_sent = [sem(f"y_sent{u}") for u in range(UN)]
        lower_in = [sem(f"lower_in{G}") for G in range(NG)]
        higher_in = [sem(f"higher_in{G}") for G in range(NG)]
        lower_added = sem("lower_added")
        out_ready, stored = sem("out_ready"), sem("stored")

        block = ctx.enter_context(nc.Block())

        def item(stage, G, n=0):
            return ITEM[(stage, G, n)] + 1

        def bank(stage, G, n=0):
            return wk[ITEM[(stage, G, n)] % BR]

        def keys_of(G):
            return slice(G % KR * GQ, (G % KR + 1) * GQ)

        def values_of(G):
            return slice(G % VR * GT, (G % VR + 1) * GT)

        def values_at(G, kb):
            return (G // GB * GB + kb // GT) % VR * GT + kb % GT

        def wait_count(eng, semaphore, n):
            if not (isinstance(n, int) and n <= 0):
                eng.wait_ge(semaphore, n)

        def wait_rest(eng, s):
            eng.wait_ge(p_lo_pool_ready if rest_on_pool(s) else p_lo_ready, rests(s, rest_on_pool(s)))

        def expert_rounds(eng, step, un=UN):
            rounds = -(-MAXT // un)
            last = MAXT - (rounds - 1) * un
            for u in range(un):
                step(0, u, lambda k: u + k >= 0)
            with eng.Fori(1, rounds - 1) as turn:
                for u in range(un):
                    step(turn * un, u, lambda k: True)
            for u in range(last):
                step((rounds - 1) * un, u, lambda k: u + k < last)

        def results(k, G):
            return ys[k * T + G * GQ:k * T + (G + 1) * GQ, :].rearrange("(t p) d -> p t d", p=P)

        def take_rest(eng, engine, s, done):
            G = max(k for k in range(NG) if FIRST_STEP[k] <= s)
            width = steps(G % GB)[s - FIRST_STEP[G]][2]
            eng.wait_ge(p_hi_ready, s + 1)
            wait_count(eng, pv_done, s - PR + 1)
            engine.tensor_tensor(p_lo[:, s % PR, 0:width], prob[:, s % PB, 0:width],
                                 p_hi[:, s % PR, 0:width].bitcast(f32), ALU.subtract).then_inc(done, 1)

        @block.sync
        def _(sp):
            for G in range(NG):
                sp.dma_start(xs_[:, G * GT:(G + 1) * GT, :],
                             xf[G * GQ:(G + 1) * GQ, :].rearrange("(t p) d -> p t d", p=P)).then_inc(x_in[G], 16)
                if G == 0:
                    for i in range(2):
                        sp.dma_start(wq_dup[i * DH:(i + 1) * DH, :], w_qkv[0:DH, :]).then_inc(wqkv_in, 16)
                        sp.dma_start(wk_dup[i * DH:(i + 1) * DH, :], w_qkv[DH:2 * DH, :]).then_inc(wqkv_in, 16)
                    sp.dma_start(wv_[:, :], w_qkv[2 * DH:3 * DH, :]).then_inc(wqkv_in, 16)
                    sp.dma_start(wo2[:, 0:DH], w_out).then_inc(wqkv_in, 16)
                    sp.dma_start(wo2[:, DH:], w_out).then_inc(wqkv_in, 16)
                    sp.dma_start(wo_aug[DH:DH + 1, 0:D], b_out.rearrange("(a n) -> a n", a=1)).then_inc(wout_in, 16)
                    sp.dma_start(gate[:, :], gate_w).then_inc(gate_in, 16)
                    sp.dma_start(b_raw[:, 0:NB1], b1.rearrange("e f -> (e f)").rearrange("(p n) -> p n", p=P)).then_inc(b_in, 16)
                    sp.dma_start(b_raw[:, NB1:], b2.rearrange("e d -> (e d)").rearrange("(p n) -> p n", p=P)).then_inc(b_in, 16)
            for e in range(E):
                wait_count(sp, w_hi_ready, 2 * e)
                wait_count(sp, w_lo_ready, 2 * e)
                sp.dma_start(w_raw[:, 0, :], w1[e, :, :]).then_inc(w12_in, 16)
                sp.dma_start(w_raw[:, 1, :].rearrange("p (c d) -> p c d", c=FC),
                             w2[e, :, :].rearrange("(c p) d -> p c d", p=P)).then_inc(w12_in, 16)
            sp.wait_ge(bias_split, 2 * NB - 1)
            for i in range(NB):
                sp.dma_start(b1_r[i:i + 1, :], b_part[:, i, 0:NB1]).then_inc(bias_in, 16)
                sp.dma_start(b2_r[i:i + 1, :], b_part[:, i, NB1:]).then_inc(bias_in, 16)
            sp.wait_ge(consts0, N_FILLS)
            sp.dma_start(disp[E * REGION:E * REGION + P, :], pad_rows[:, :]).then_inc(padded, 16)

            def first_row(i):
                return sp.value_load(tile_row[0:1, bass.ds(i, 1)], min_val=0, max_val=E * REGION)

            sp.wait_ge(table_ready, 1)
            first_rows = [first_row(u) for u in range(3)]
            for i in range(2):
                sp.wait_ge(sent[i], 16 * TOP * GT * (NG // 2))
            sp.wait_ge(padded, 16 * (E + 1))

            def load_rows(base, u):
                at = first_rows.pop(0) if first_rows else first_row(base + u)
                wait_count(sp, meta_ready, base + (u + 1 - UN))
                wait_count(sp, xgT_full, base + (u + 1 - UN))
                sp.dma_start(xg[:, u, :], disp[bass.ds(at, P), :]).then_inc(xg_in[u], 16)

            for u in range(UN):
                load_rows(0, u)
            with sp.Fori(1, ROUNDS - 1) as turn:
                for u in range(UN):
                    load_rows(turn * UN, u)
            for u in range(LAST):
                load_rows((ROUNDS - 1) * UN, u)

            sp.wait_ge(lanes_ready, 1)
            lane_counts = [sp.value_load(lane_wait[0:1, u:u + 1], min_val=16, max_val=16 * ROUNDS) for u in range(UN)]
            for u in range(UN):
                sp.wait_ge(y_sent[u], lane_counts[u])
            for G in range(NG):
                sp.dma_start(lower[G], results(0, G)).then_inc(lower_in[G], 16)
            for u in range(UN):
                sp.wait_ge(y_sent[u], 16 * (ROUNDS if u < LAST else ROUNDS - 1))
            for G in range(NG):
                if G >= NG - 2:
                    sp.wait_ge(lower_added, G - NG + 3)
                sp.dma_start(higher[G], results(1, G)).then_inc(higher_in[G], 16)

        @block.gpsimd
        def _(pool):
            g = nc.gpsimd
            g.memset(wo_aug[0:DH, D:D + 1], 0.0).then_inc(consts0, 1)
            g.memset(ident[:, :], 0.0).then_inc(consts0, 1)
            g.memset(mask_kq[:, :], 0.0).then_inc(consts0, 1)
            g.memset(mask_qk[:, :], 0.0).then_inc(consts0, 1)
            g.memset(tri[:, :], 1.0).then_inc(consts0, 1)
            g.memset(incl[:, :, :], 1.0).then_inc(consts0, 1)
            g.memset(ones_b[:, :], 1.0).then_inc(consts0, 1)
            g.memset(sum_col[:, 0:DH].bitcast(f32), 0.0).then_inc(consts0, 1)
            g.memset(sum_col[:, DH:DH + 1].bitcast(f32), 1.0).then_inc(consts0, 1)
            g.memset(wo_dup[:, D:D + 1], 0.0).then_inc(consts0, 1)
            g.memset(mhalf[:, :], -0.5).then_inc(consts0, 1)
            g.memset(mneg[:, :, :].bitcast(f32), 0.0).then_inc(consts0, 1)
            g.memset(V[:, :, 2 * DH:].bitcast(f32), 1.0).then_inc(consts0, 1)
            g.memset(both[:, 0, 0], 0.0).then_inc(consts0, 1)
            g.memset(pad_rows[:, 0:D + 1], 0.0).then_inc(consts0, 1)
            g.memset(pad_rows[:, D + 1:ROW], float(FAR)).then_inc(consts0, 1)
            g.iota(tile_no_i[:, :], [[1, MAXT]], base=0, channel_multiplier=0).then_inc(consts0, 1)
            g.iota(expert_i[:, :], [[1, E]], base=0, channel_multiplier=0).then_inc(consts0, 1)
            g.iota(token_i[:, :, :], [[T, TOP], [P, NT]], base=0, channel_multiplier=1).then_inc(consts0, 1)
            pool.wait_ge(consts0, N_FILLS)
            g.affine_select(out=ident[:, :], in_=ident[:, :], compare_op=ALU.not_equal, fill=1.0, base=0,
                            pattern=[[-1, P]], channel_multiplier=1).then_inc(consts, 1)
            g.affine_select(out=mask_kq[:, :], in_=mask_kq[:, :], compare_op=ALU.is_ge, fill=NEG, base=0,
                            pattern=[[1, P]], channel_multiplier=-1).then_inc(consts, 1)
            g.affine_select(out=mask_qk[:, :], in_=mask_qk[:, :], compare_op=ALU.is_ge, fill=NEG, base=0,
                            pattern=[[-1, P]], channel_multiplier=1).then_inc(consts, 1)
            g.affine_select(out=tri[:, :], in_=tri[:, :], compare_op=ALU.is_gt, fill=0.0, base=0,
                            pattern=[[1, P]], channel_multiplier=-1).then_inc(consts, 1)
            g.affine_select(out=incl[:, :, :], in_=incl[:, :, :], compare_op=ALU.is_ge, fill=0.0, base=0,
                            pattern=[[1, E], [-1, E]], channel_multiplier=0).then_inc(consts, 1)
            g.tensor_copy(tile_no[:, :], tile_no_i[:, :]).then_inc(consts, 1)
            g.tensor_copy(token_no[:, :, :], token_i[:, :, :]).then_inc(consts, 1)
            g.tensor_copy(expert_id[:, :], expert_i[:, :]).then_inc(consts, 1)
            pool.wait_ge(consts, 1)
            g.tensor_copy(ident_r[:, :], ident[:, :]).then_inc(consts, 1)
            g.tensor_copy(ident_b[:, :], ident[:, :]).then_inc(consts, 1)

            for stage, G, n in SCHEDULE:
                r = G % 2
                if stage == "LN1":
                    pool.wait_ge(var_ready, G + 1)
                    wait_count(pool, xn_ready, G)
                    g.tensor_tensor(rstd[:, :], veps[:, :], mhalf[:, :], ALU.pow).then_inc(rstd_ready, 1)
                elif stage == "LN2":
                    pool.wait_ge(var2_ready, G + 1)
                    wait_count(pool, x2n_ready, G)
                    g.tensor_tensor(rstd2[:, :], veps2[:, :], mhalf[:, :], ALU.pow).then_inc(rstd2_ready, 1)
                elif stage == "WS":
                    pool.wait_ge(w_hi_ready, 2 * (G + 1))
                    g.tensor_tensor(w1p[:, G, 1], w_raw[:, 0], w1p[:, G, 0].bitcast(f32),
                                    ALU.subtract).then_inc(w_lo_ready, 1)
                    g.tensor_tensor(w2p[:, G, :, 1], w_raw[:, 1].rearrange("p (c d) -> p c d", c=FC),
                                    w2p[:, G, :, 0].bitcast(f32), ALU.subtract).then_inc(w_lo_ready, 1)
                elif stage == "AS":
                    s = FIRST_STEP[G] + n
                    if rest_on_pool(s):
                        take_rest(pool, g, s, p_lo_pool_ready)
                elif stage == "SC":
                    if n == 0:
                        pool.wait_ge(slots_ready, G + 1)
                        pool.wait_ge(copies_ready, G + 1)
                    for k in range(TOP):
                        g.indirect_dma_start(
                            out=disp, out_offset=bass.IndirectOffsetOnAxis(ap=slot[:, r, k, n:n + 1], axis=0),
                            in_=rows[:, r, n, k, :], in_offset=None).then_inc(sent[r], 16)

            bound = pool.to_reg(NSLOT - 1)

            def step(base, u, has):
                pool.wait_ge(y_ready, base + u + 1)
                pool.sem_inc(scatters_begun, 1)
                g.indirect_dma_start(
                    out=ys, out_offset=bass.IndirectOffsetOnAxis(ap=goes_to[:, u:u + 1], axis=0),
                    in_=y[:, u, :], in_offset=None, bounds_check=bound, oob_is_err=False).then_inc(y_sent[u], 16)

            expert_rounds(pool, step)

        @block.scalar
        def _(act):
            a = nc.scalar
            copy = ACT.Copy
            act.wait_ge(wT_ready, 1)
            a.activation(wqT[:, :], st[0][:, 0:P], copy).then_inc(wT_copied, 1)
            a.activation(wkT[:, :], st[0][:, P:2 * P], copy).then_inc(wT_copied, 1)
            a.activation(wvT[:, :], st[0][:, 2 * P:2 * P + DH], copy).then_inc(wT_copied, 1)
            a.activation(wo_aug[0:DH, 0:D], st[0][0:DH, 3 * P:4 * P], copy).then_inc(wT_copied, 1)
            a.activation(wo_dup[:, 0:D], st[0][:, 3 * P:4 * P], copy).then_inc(wT_copied, 1)

            for stage, G, n in ACT_ORDER:
                r = G % 2
                if stage in READERS and "a" in READERS[stage]:
                    act.wait_ge(bank_full, item(stage, G, n))
                    ps = bank(stage, G, n)
                if stage == "XT":
                    if G >= 2:
                        act.wait_ge(bank_full, item("VP", G - 2))
                    a.activation(xT[:, r], ps[:, :], copy).then_inc(bank_act, 1)
                elif stage == "QP":
                    if G >= QR:
                        act.wait_ge(scores_ready, FIRST_STEP[G - QR + 1])
                    a.activation(q_hi[:, G % QR], ps[:, :], copy).then_inc(bank_act, 1)
                elif stage == "KP":
                    if G >= KR:
                        act.wait_ge(scores_ready, FIRST_STEP[GB])
                    a.activation(k_hl[:, keys_of(G)], ps[:, :], copy).then_inc(k_hi_ready, 1)
                    a.activation(k_h1[0:DH, keys_of(G)], ps[0:DH, :], copy).then_inc(bank_act, 1)
                elif stage == "VP":
                    if G >= VR:
                        act.wait_ge(pv_done, FIRST_STEP[GB])
                    a.activation(V[:, values_of(G), DH:2 * DH],
                                 ps[:, 0:GT * DH].rearrange("p (t d) -> p t d", t=GT), copy).then_inc(bank_act, 1)
                elif stage == "WS":
                    act.wait_ge(w12_in, 32 * (G + 1))
                    a.activation(w1p[:, G, 0], w_raw[:, 0], copy).then_inc(w_hi_ready, 1)
                    a.activation(w2p[:, G, :, 0], w_raw[:, 1].rearrange("p (c d) -> p c d", c=FC),
                                 copy).then_inc(w_hi_ready, 1)
                elif stage == "MR":
                    if G >= QR:
                        act.wait_ge(scores_ready, FIRST_STEP[G - QR + 1])
                    a.activation(q_lo[DH:DH + 1, G % QR, :], ps[DH:DH + 1, :], copy).then_inc(bank_act, 1)
                elif stage == "AS":
                    s = FIRST_STEP[G] + n
                    act.wait_ge(scores_ready, s + 1)
                    if s >= PB:
                        wait_rest(act, s - PB)
                    width = steps(G % GB)[n][2]
                    a.activation(prob[:, s % PB, 0:width], st[s % BR][:, 0:width], ACT.Exp,
                                 scale=SCALE).then_inc(probs_ready, 1)
                    wait_count(act, pv_done, s - PR + 1)
                    a.activation(p_hi[:, s % PR, 0:width], st[s % BR][:, 0:width], ACT.Exp,
                                 scale=SCALE).then_inc(p_hi_ready, 1)
                elif stage == "OE":
                    act.wait_ge(pv_done, FIRST_STEP[G + 1])
                    if G >= 1:
                        act.wait_ge(bank_full, item("OP", G - 1, 1))
                    a.activation(oA[:, :], pv[0][:, :], copy).then_inc(o_ready, 1)
                    a.activation(oB[:, :], pv[1][0:DH + 1, :], copy).then_inc(o_ready, 1)
                elif stage == "X2T":
                    if G >= 1:
                        act.wait_ge(bank_full, item("LG", G - 1))
                    a.activation(x2T[:, :], ps[:, :], copy).then_inc(bank_act, 1)
                elif stage == "RT":
                    act.wait_ge(gap_ready, G + 1)
                    a.activation(egap[:, :], gap[:, :], ACT.Exp).then_inc(egap_ready, 1)
                    act.wait_ge(x2n_ready, G + 1)
                    a.activation(rows[:, r, :, 1, 0:D], rows[:, r, :, 0, 0:D], copy).then_inc(copies_ready, 1)

            act.wait_ge(pad_at_ready, 1)
            for at in [act.value_load(pad_at[0:1, e:e + 1], min_val=e * REGION, max_val=e * REGION + T) for e in range(E)]:
                act.dma_start(disp[bass.ds(at, P), :], pad_rows[:, :]).then_inc(padded, 16)

            def take_gelu(base, k):
                act.wait_ge(h_full, base + k + 1)
                wait_count(act, hT_full, base + (k - 1))
                a.activation(h[:, k % 2], h_ps[k % 2][:, :], ACT.Gelu).then_inc(h_ready, 1)

            def weigh(base, k):
                act.wait_ge(y_full, base + k + 1)
                a.activation(y[:, k % UN], pv[k % 2][:, D:2 * D], copy,
                             scale=weight[:, k % UN:k % UN + 1]).then_inc(y_rest_ready, 1)

            def step(base, u, has):
                if has(1):
                    take_gelu(base, u + 1)
                if has(-2):
                    weigh(base, u - 2)
                act.wait_ge(hT_full, base + u + 1)
                wait_count(act, y_full, base + (u + 1 - XR))
                a.activation(hT_hi[:, u % XR], hT_ps[u % 2][:, :], copy).then_inc(hT_hi_ready, 1)

            take_gelu(0, 0)
            expert_rounds(act, step)
            for k in (LAST - 2, LAST - 1):
                weigh((ROUNDS - 1) * UN, k)

            for G in range(NG):
                act.wait_ge(out_ready, G + 1)
                act.dma_start(of[G * GQ:(G + 1) * GQ, :].rearrange("(t p) d -> p t d", p=P),
                              xs_[:, G * GT:(G + 1) * GT, :]).then_inc(stored, 16)
            act.wait_ge(stored, 16 * NG)

        @block.vector
        def _(dve):
            v = nc.vector
            links = [0]

            def link(ins):
                links[0] += 1
                ins.then_inc(vec, 1)
                dve.wait_ge(vec, links[0])

            v.memset(wo_aug[DH:DH + 1, D:D + 1], 1.0).then_inc(consts0, 1)
            v.memset(k_h1[DH:DH + 1, :].bitcast(f32), 1.0).then_inc(consts0, 1)

            def layernorm_stats(G, stats_of, mv_of, veps_of, ready):
                for t in range(GT):
                    ins = v.bn_stats(stats_of[:, t], xs_[:, G * GT + t])
                    if t < GT - 1:
                        ins.then_inc(vec, 1)
                        links[0] += 1
                link(ins)
                for t in range(GT):
                    ins = v.bn_aggr(mv_of[:, t], stats_of[:, t])
                    if t < GT - 1:
                        ins.then_inc(vec, 1)
                        links[0] += 1
                link(ins)
                v.tensor_scalar(veps_of[:, :], mv_of[:, :, 1], EPS, None, ALU.add).then_inc(ready, 1)

            for stage, G, n in DVE_ORDER:
                r, tiles = G % 2, slice(G * GT, (G + 1) * GT)
                if stage in READERS and "v" in READERS[stage]:
                    dve.wait_ge(bank_full, item(stage, G, n))
                    ps = bank(stage, G, n)
                if stage == "LN1":
                    dve.wait_ge(x_in[G], 16)
                    wait_count(dve, xn_ready, G)
                    wait_count(dve, rstd_ready, G)
                    layernorm_stats(G, stats, mv, veps, var_ready)
                elif stage == "BIAS":
                    dve.wait_ge(b_in, 32)
                    for i in range(NB):
                        v.tensor_copy(b_part[:, i], b_raw[:, :]).then_inc(bias_split, 1)
                        dve.wait_ge(bias_split, 2 * i + 1)
                        if i < NB - 1:
                            v.tensor_tensor(b_raw[:, :], b_raw[:, :], b_part[:, i], ALU.subtract).then_inc(bias_split, 1)
                            dve.wait_ge(bias_split, 2 * i + 2)
                elif stage == "NORM1":
                    dve.wait_ge(rstd_ready, G + 1)
                    if G >= 2:
                        dve.wait_ge(bank_full, item("XT", G - 2))
                    for t in range(GT):
                        ins = v.tensor_scalar(xn[:, r, t], xs_[:, G * GT + t], mv[:, t, 0:1], rstd[:, t:t + 1],
                                              ALU.subtract, ALU.mult)
                        if t < GT - 1:
                            ins.then_inc(vec, 1)
                            links[0] += 1
                    ins.then_inc(xn_ready, 1)
                elif stage == "QP":
                    dve.wait_ge(bank_act, ACT_READS[item(stage, G) - 1])
                    if G >= QR:
                        dve.wait_ge(scores_ready, FIRST_STEP[G - QR + 1])
                    v.tensor_tensor(q_lo[0:DH, G % QR], ps[0:DH, :], q_hi[0:DH, G % QR].bitcast(f32),
                                    ALU.subtract).then_inc(bank_dve, 1)
                elif stage == "KP":
                    dve.wait_ge(k_hi_ready, G + 1)
                    v.tensor_tensor(k_hl[DH:P, keys_of(G)], ps[DH:P, :], k_hl[DH:P, keys_of(G)].bitcast(f32),
                                    ALU.subtract).then_inc(bank_dve, 1)
                elif stage == "VP":
                    dve.wait_ge(bank_act, ACT_READS[item(stage, G) - 1])
                    v.tensor_tensor(V[:, values_of(G), 0:DH], ps[:, 0:GT * DH].rearrange("p (t d) -> p t d", t=GT),
                                    V[:, values_of(G), DH:2 * DH].bitcast(f32), ALU.subtract).then_inc(bank_dve, 1)
                elif stage == "AS":
                    s = FIRST_STEP[G] + n
                    for k in [s - 1] * (s > 0) + [s] * (s == FIRST_STEP[NG] - 1):
                        if not rest_on_pool(k):
                            take_rest(dve, v, k, p_lo_ready)
                elif stage == "MX":
                    t, c = n
                    g = G % GB
                    if n == (0, 0):
                        wait_count(dve, mneg_ready, G)
                    width = GQ if c < g else (t + 1) * P
                    v.tensor_reduce(mpart[:, t, c:c + 1], ps[:, 0:width], AX.X, ALU.max).then_inc(bank_dve, 1)
                elif stage == "MR":
                    g = G % GB
                    dve.wait_ge(bank_dve, DVE_READS[item("MX", G, (GT - 1, g)) - 1])
                    if G >= 1:
                        dve.wait_ge(bank_full, item("MR", G - 1))
                    else:
                        dve.wait_ge(consts0, N_FILLS)
                    v.tensor_reduce(mneg[:, :, DH], mpart[:, :, 0:g + 1], AX.X, ALU.max,
                                    negate=True).then_inc(mneg_ready, 1)
                elif stage == "OP":
                    both_tiles = ps[:, 0:2 * (D + 1)].rearrange("p (t d) -> p t d", t=2)
                    if G or n:
                        dve.wait_ge(bank_dve, DVE_READS[item("OP", *((G, 0) if n else (G - 1, 1))) - 1])
                    link(v.reciprocal(rsum[:, :], both_tiles[:, :, D]))
                    for t in range(2):
                        tile = G * GT + 2 * n + t
                        if t == 0 and n == 0:
                            dve.wait_ge(xn_ready, G + 1)
                        ins = v.scalar_tensor_tensor(xs_[:, tile], both_tiles[:, t, 0:D], rsum[:, t:t + 1],
                                                     xs_[:, tile], ALU.mult, ALU.add)
                        if t == 0:
                            ins.then_inc(x2_ready, 1)
                    ins.then_inc(bank_dve, 1)
                elif stage == "LN2":
                    dve.wait_ge(bank_dve, DVE_READS[item("OP", G, 1) - 1])
                    dve.wait_ge(x2_ready, 2 * G + 2)
                    wait_count(dve, x2n_ready, G)
                    wait_count(dve, rstd2_ready, G)
                    layernorm_stats(G, stats, mv2, veps2, var2_ready)
                elif stage == "NORM2":
                    dve.wait_ge(rstd2_ready, G + 1)
                    if G >= 2:
                        dve.wait_ge(sent[r], 16 * TOP * GT * (G // 2))
                    for t in range(GT):
                        ins = v.tensor_scalar(rows[:, r, t, 0, 0:D], xs_[:, G * GT + t], mv2[:, t, 0:1],
                                              rstd2[:, t:t + 1], ALU.subtract, ALU.mult)
                        if t < GT - 1:
                            ins.then_inc(vec, 1)
                            links[0] += 1
                    ins.then_inc(x2n_ready, 1)
                elif stage == "LG":
                    wait_count(dve, slots_ready, G)
                    logits = ps[:, 0:GT * E].rearrange("p (t e) -> p t e", t=GT)
                    for t in range(GT):
                        v.max(top8[:, t], logits[:, t]).then_inc(vec, 1)
                    for t in range(GT):
                        dve.wait_ge(vec, links[0] + t + 1)
                        ins = v.max_index(top_i[:, t], top8[:, t], logits[:, t])
                        if t < GT - 1:
                            ins.then_inc(vec, 1)
                    links[0] += 2 * GT - 1
                    ins.then_inc(bank_dve, 1)
                    wait_count(dve, egap_ready, G)
                    v.tensor_tensor(gap[:, :], top8[:, :, 1], top8[:, :, 0], ALU.subtract).then_inc(gap_ready, 1)
                    dve.wait_ge(vec, links[0])
                    dve.wait_ge(bank_dve, DVE_READS[item("LG", G) - 1])
                    link(v.tensor_copy(top_f[:, :, :], top_i[:, :, 0:TOP]))
                    link(v.tensor_tensor(pick[:, :, :, :],
                                         expert_id[:, :].unsqueeze(1).unsqueeze(1).to_broadcast((P, TOP, GT, E)),
                                         top_f[:, :, :].rearrange("p t k -> p k t").unsqueeze(3).to_broadcast((P, TOP, GT, E)),
                                         ALU.is_equal))
                    v.tensor_tensor(both[:, r, 1:], pick[:, 0], pick[:, 1], ALU.add).then_inc(picks_ready, 1)
                elif stage == "RT":
                    dve.wait_ge(egap_ready, G + 1)
                    link(v.tensor_scalar(veps2[:, :], egap[:, :], 1.0, None, ALU.add))
                    link(v.reciprocal(rows[:, r, :, 0, D], veps2[:, :]))
                    link(v.tensor_tensor(rows[:, r, :, 1, D], egap[:, :], rows[:, r, :, 0, D], ALU.mult))
                    link(v.tensor_tensor(second[:, :], top_f[:, :, 0], top_f[:, :, 1], ALU.is_gt))
                    for k in range(TOP):
                        ins = v.scalar_tensor_tensor(rows[:, r, :, k, D + 1], second[:, :],
                                                     float(-T if k else T), token_no[:, k, tiles], ALU.mult, ALU.add)
                        if k == 0:
                            ins.then_inc(vec, 1)
                            links[0] += 1
                    link(ins)
                elif stage == "RK":
                    ranks = ps[:, 0:GT * E].rearrange("p (t e) -> p t e", t=GT)
                    v.tensor_tensor(ranked[:, :, :, :], pick[:, :, :, :],
                                    ranks.unsqueeze(1).to_broadcast((P, TOP, GT, E)), ALU.mult).then_inc(bank_dve, 1)
                    with nc.allow_low_precision(reason="a partition's counts are at most NT, exact in bfloat16"):
                        v.tensor_reduce(both[:, 1 - r, 0], both[:, r].rearrange("p t e -> p e t"), AX.X,
                                        ALU.add).then_inc(seen_ready, 1)
                    dve.wait_ge(bank_dve, DVE_READS[item("RK", G) - 1])
                    link(v.tensor_reduce(slot_f[:, :, :], ranked[:, :, :, :], AX.X, ALU.add))
                    v.scalar_tensor_tensor(slot[:, r], top_f[:, :, :].rearrange("p t k -> p k t"), float(REGION),
                                           slot_f[:, :, :], ALU.mult, ALU.add).then_inc(slots_ready, 1)
                elif stage == "CN":
                    link(v.tensor_copy(cnt[:, :], ps[:, 0:E]))
                    v.scalar_tensor_tensor(pad_at[:, :], expert_id[:, :], float(REGION), cnt[:, :],
                                           ALU.mult, ALU.add).then_inc(pad_at_ready, 1)
                    link(v.tensor_scalar(cnt_i[:, :], cnt[:, :], float(P - 1), None, ALU.add))
                    link(v.tensor_scalar(nt_i[:, :], cnt_i[:, :], P.bit_length() - 1, None, ALU.logical_shift_right))
                    link(v.tensor_copy(nt_f[:, :], nt_i[:, :]))
                    link(v.tensor_tensor(cum8[:, :, :], incl[:, :, :],
                                         nt_f[:, :].unsqueeze(1).to_broadcast((P, E, E)), ALU.mult))
                    link(v.tensor_reduce(cend[:, :], cum8[:, :, :], AX.X, ALU.add))
                    link(v.tensor_scalar(skip[:, :], nt_f[:, :], -float(P), float(REGION), ALU.mult, ALU.add))
                    link(v.tensor_tensor(past[:, :, :], tile_no[:, :].unsqueeze(2).to_broadcast((P, MAXT, E)),
                                         cend[:, :].unsqueeze(1).to_broadcast((P, MAXT, E)), ALU.is_ge))
                    link(v.tensor_reduce(te_f[:, :], past[:, :, :], AX.X, ALU.add))
                    link(v.tensor_scalar(tile_expert[:, :], te_f[:, :], float(E - 1), None, ALU.min))
                    link(v.tensor_tensor(past2[:, :, :], past[:, :, :],
                                         skip[:, :].unsqueeze(1).to_broadcast((P, MAXT, E)), ALU.mult))
                    link(v.tensor_reduce(tr_f[:, :], past2[:, :, :], AX.X, ALU.add))
                    link(v.scalar_tensor_tensor(te_f[:, :], tile_no[:, :], float(P), tr_f[:, :], ALU.mult, ALU.add))
                    v.tensor_scalar(tile_row[:, :], te_f[:, :], float(E * REGION), None,
                                    ALU.min).then_inc(table_ready, 1)
                    link(v.scalar_tensor_tensor(lane_f[:, :], tile_no[:, 0:UN], -1.0,
                                                cend[:, E - 2:E - 1].to_broadcast((P, UN)), ALU.mult, ALU.add))
                    link(v.tensor_scalar(lane_i[:, :], lane_f[:, :], float(UN - 1), float(UN), ALU.add, ALU.max))
                    link(v.tensor_scalar(lane_i[:, :], lane_i[:, :], UN.bit_length() - 1, None, ALU.logical_shift_right))
                    v.tensor_scalar(lane_wait[:, :], lane_i[:, :], 16.0, None, ALU.mult).then_inc(lanes_ready, 1)

            def take_rows(base, k):
                dve.wait_ge(xgT_full, base + k + 1)
                wait_count(dve, h_full, base + (k + 1 - XR))
                ps = wk[k % 2][:, 0:P]
                v.tensor_copy(xgT_hi[:, k % XR], ps).then_inc(xgT_hi_ready, 1)
                wait_count(dve, y_sent[k % UN], (16 // UN) * base + 16 * (k // UN))
                v.tensor_copy(weight[:, k % UN:k % UN + 1], xg[:, k % UN, D:D + 1])
                v.tensor_copy(goes_to[:, k % UN:k % UN + 1], xg[:, k % UN, D + 1:ROW]).then_inc(meta_ready, 1)
                dve.wait_ge(xgT_hi_ready, base + k + 1)
                v.tensor_tensor(xgT_lo[:, k % XR], ps, xgT_hi[:, k % XR].bitcast(f32),
                                ALU.subtract).then_inc(xgT_ready, 1)

            def weigh(base, k):
                dve.wait_ge(y_rest_ready, base + k + 1)
                v.scalar_tensor_tensor(y[:, k % UN], pv[k % 2][:, 0:D], weight[:, k % UN:k % UN + 1], y[:, k % UN],
                                       ALU.mult, ALU.add).then_inc(y_ready, 1)

            def step(base, u, has):
                if has(3):
                    take_rows(base, u + 3)
                if has(-2):
                    weigh(base, u - 2)
                dve.wait_ge(hT_hi_ready, base + u + 1)
                wait_count(dve, y_full, base + (u + 1 - XR))
                v.tensor_tensor(hT_lo[:, u % XR], hT_ps[u % 2][:, :],
                                hT_hi[:, u % XR].bitcast(f32), ALU.subtract).then_inc(hT_ready, 1)

            for k in range(3):
                take_rows(0, k)
            expert_rounds(dve, step)
            for k in (LAST - 2, LAST - 1):
                weigh((ROUNDS - 1) * UN, k)

            for parts, arrived, done in ((lower, lower_in, lower_added), (higher, higher_in, out_ready)):
                for G in range(NG):
                    tiles = slice(G * GT, (G + 1) * GT)
                    dve.wait_ge(arrived[G], 16)
                    if done is out_ready:
                        dve.wait_ge(lower_added, G + 1)
                    v.tensor_tensor(xs_[:, tiles], xs_[:, tiles], parts[G], ALU.add).then_inc(done, 1)

        @block.tensor
        def _(pe):
            t_ = nc.tensor

            def free_bank(stage, G, n):
                k = ITEM[(stage, G, n)]
                if k >= BR:
                    wait_count(pe, bank_act, ACT_READS[k - BR])
                    wait_count(pe, bank_dve, DVE_READS[k - BR])
                return bank(stage, G, n)

            pe.wait_ge(wqkv_in, 112)
            pe.wait_ge(consts, N_CONSTS)
            t_.transpose(st[0][:, 0:P], wq_dup[:, :], ident[:, :])
            t_.transpose(st[0][:, P:2 * P], wk_dup[:, :], ident[:, :])
            t_.transpose(st[0][:, 2 * P:2 * P + DH], wv_[:, :], ident[0:DH, 0:DH])
            t_.transpose(st[0][:, 3 * P:4 * P], wo2[:, :], ident[:, :]).then_inc(wT_ready, 1)

            def product_with_v(s):
                G = max(k for k in range(NG) if FIRST_STEP[k] <= s)
                n = s - FIRST_STEP[G]
                blocks = steps(G % GB)
                wait_rest(pe, s)
                if n == 0:
                    wait_count(pe, o_ready, 2 * G)
                kb, q0, w = blocks[n]
                first, last = n == 0, n == len(blocks) - 1
                vt = values_at(G, kb)
                hi, lo = p_hi[:, s % PR, 0:w], p_lo[:, s % PR, 0:w]
                t_.matmul(pv[0][:, q0:q0 + w], V[:, vt, 0:2 * DH], hi, start=first, stop=last)
                t_.matmul(pv[1][0:DH + 1, q0:q0 + w], V[:, vt, DH:2 * DH + 1], lo, start=first, stop=False)
                ins = t_.matmul(pv[1][0:DH + 1, q0:q0 + w], sum_col[:, :], hi, start=False, stop=last)
                ins.then_inc(pv_done, 1)

            for stage, G, n in SCHEDULE:
                r, b, g = G % 2, G // GB, G % GB
                if stage in READERS:
                    ps = free_bank(stage, G, n)
                if stage == "XT":
                    pe.wait_ge(xn_ready, G + 1)
                    for t in range(GT):
                        ins = t_.transpose(ps[:, t * P:(t + 1) * P], xn[:, r, t], ident[:, :])
                    ins.then_inc(bank_full, 1)
                elif stage in ("QP", "KP"):
                    if stage == "QP":
                        pe.wait_ge(wT_copied, 5)
                        pe.wait_ge(bank_act, ACT_READS[item("XT", G) - 1])
                    t_.matmul(ps[:, :], (wqT if stage == "QP" else wkT)[:, :], xT[:, r], start=True,
                              stop=True).then_inc(bank_full, 1)
                elif stage == "VP":
                    for t in range(GT):
                        ins = t_.matmul(ps[:, t * DH:(t + 1) * DH], xT[:, r, t * P:(t + 1) * P], wvT[:, :],
                                        start=True, stop=True)
                    ins.then_inc(bank_full, 1)
                elif stage == "MX":
                    t, c = n
                    width = GQ if c < g else (t + 1) * P
                    k0 = keys_of(b * GB + c).start
                    if n == (0, 0):
                        pe.wait_ge(bank_act, ACT_READS[item("QP", G) - 1])
                        pe.wait_ge(bank_dve, DVE_READS[item("KP", G) - 1])
                    ins = t_.matmul(ps[:, 0:width], q_hi[:, G % QR, t * P:(t + 1) * P], k_hl[:, k0:k0 + width],
                                    start=True, stop=(c < g))
                    if c == g:
                        ins = t_.matmul(ps[:, width - P:width], ident_b[:, :], mask_qk[:, :], start=False, stop=True)
                    ins.then_inc(bank_full, 1)
                elif stage == "MR":
                    pe.wait_ge(mneg_ready, G + 1)
                    for t in range(GT):
                        ins = t_.matmul(ps[0:DH + 1, t * P:(t + 1) * P], mneg[:, t, 0:DH + 1], ident_r[:, :],
                                        start=True, stop=True)
                    ins.then_inc(bank_full, 1)
                elif stage == "AS":
                    s = FIRST_STEP[G] + n
                    if n == 0:
                        pe.wait_ge(bank_act, ACT_READS[item("MR", G) - 1])
                        pe.wait_ge(bank_dve, DVE_READS[item("QP", G) - 1])
                    wait_count(pe, p_hi_ready, s - BR + 1)
                    kb, q0, w = steps(g)[n]
                    k0 = keys_of(b * GB + kb // GT).start + kb % GT * P
                    diagonal = kb >= GT * g
                    o = st[s % BR]
                    t_.matmul(o[:, 0:w], k_hl[:, k0:k0 + P], q_hi[:, G % QR, q0:q0 + w], start=True, stop=False)
                    ins = t_.matmul(o[:, 0:w], k_h1[:, k0:k0 + P], q_lo[:, G % QR, q0:q0 + w],
                                    start=False, stop=not diagonal)
                    if diagonal:
                        ins = t_.matmul(o[:, 0:P], ident_b[:, :], mask_kq[:, :], start=False, stop=True)
                    ins.then_inc(scores_ready, 1)
                    if s >= LAG:
                        product_with_v(s - LAG)
                elif stage == "AE":
                    product_with_v(FIRST_STEP[NG] - LAG + n)
                elif stage == "OP":
                    pe.wait_ge(o_ready, 2 * (G + 1))
                    pe.wait_ge(wout_in, 16)
                    for t in range(2):
                        q0 = (2 * n + t) * P
                        o = ps[:, t * (D + 1):(t + 1) * (D + 1)]
                        t_.matmul(o, oA[:, q0:q0 + P], wo_dup[:, :], start=True, stop=False)
                        ins = t_.matmul(o, oB[:, q0:q0 + P], wo_aug[:, :], start=False, stop=True)
                    ins.then_inc(bank_full, 1)
                elif stage == "X2T":
                    pe.wait_ge(x2n_ready, G + 1)
                    for t in range(GT):
                        ins = t_.transpose(ps[:, t * P:(t + 1) * P], rows[:, r, t, 0, 0:D], ident[:, :])
                    ins.then_inc(bank_full, 1)
                elif stage == "LG":
                    pe.wait_ge(gate_in, 16)
                    pe.wait_ge(bank_act, ACT_READS[item("X2T", G) - 1])
                    for t in range(GT):
                        ins = t_.matmul(ps[:, t * E:(t + 1) * E], x2T[:, t * P:(t + 1) * P], gate[:, :],
                                        start=True, stop=True)
                    ins.then_inc(bank_full, 1)
                elif stage == "RK":
                    pe.wait_ge(picks_ready, G + 1)
                    wait_count(pe, seen_ready, G)
                    for t in range(GT):
                        o = ps[:, t * E:(t + 1) * E]
                        for before in range(t + 1):
                            t_.matmul(o, ones_b[:, :], both[:, r, before], start=(before == 0), stop=False)
                        ins = t_.matmul(o, tri[:, :], both[:, r, t + 1], start=False, stop=True)
                    ins.then_inc(bank_full, 1)
                elif stage == "CN":
                    pe.wait_ge(seen_ready, NG)
                    t_.matmul(ps[:, 0:E], ones_b[:, :], both[:, NG % 2, 0], start=True, stop=True).then_inc(bank_full, 1)

            def transpose_rows(base, k):
                pe.wait_ge(xg_in[k % UN], (16 // UN) * base + 16 * (k // UN + 1))
                wait_count(pe, xgT_ready, base + (k - 1))
                t_.transpose(wk[k % 2][:, 0:P], xg[:, k % UN, 0:D], ident[:, :]).then_inc(xgT_full, 1)

            experts = {}
            carried = [pe.alloc_register(f"carried_expert{i}") for i in range(3)]

            def expert(base, k):
                key = (str(base), k)
                if key not in experts:
                    if k <= 0 and not (isinstance(base, int) and base == 0):
                        experts[key] = pe.snap(carried[k + 2], min_val=0, max_val=E - 1)
                    else:
                        experts[key] = pe.value_load(tile_expert[0:1, bass.ds(base + k, 1)], min_val=0, max_val=E - 1)
                return experts[key]

            def first_product(base, k):
                e = expert(base, k)
                pe.wait_ge(xgT_ready, base + k + 1)
                wait_count(pe, h_ready, base + (k - 1))
                o = h_ps[k % 2][:, :]
                hi, lo = xgT_hi[:, k % XR], xgT_lo[:, k % XR]
                w_hi, w_lo = (w1p[:, bass.ds(e, 1), i].rearrange("p a f -> p (a f)") for i in range(2))
                t_.matmul(o, hi, w_hi, start=True, stop=False)
                t_.matmul(o, hi, w_lo, start=False, stop=False)
                t_.matmul(o, lo, w_hi, start=False, stop=False)
                t_.matmul(o, ones_b[0:NB, :], b1_r[:, bass.ds(e * F, F)], start=False, stop=True).then_inc(h_full, 1)

            def second_product(base, k):
                e = expert(base, k)
                pe.wait_ge(hT_ready, base + k + 1)
                wait_count(pe, y_ready, base + (k - 1))
                for c in range(FC):
                    hi, lo = (t[:, k % XR, c * P:(c + 1) * P] for t in (hT_hi, hT_lo))
                    w = w2p[:, bass.ds(e, 1), c]
                    t_.matmul(pv[k % 2][:, 0:2 * D], hi, w.rearrange("p a i d -> p (a i d)"), start=(c == 0), stop=False)
                    t_.matmul(pv[k % 2][:, 0:D], lo, w[:, :, 0].rearrange("p a d -> p (a d)"), start=False, stop=False)
                t_.matmul(pv[k % 2][:, 0:D], ones_b[0:NB, :], b2_r[:, bass.ds(e * D, D)], start=False,
                          stop=True).then_inc(y_full, 1)

            def step(base, u, has):
                if has(1):
                    first_product(base, u + 1)
                if has(3):
                    transpose_rows(base, u + 3)
                if has(-2):
                    second_product(base, u - 2)
                pe.wait_ge(h_ready, base + u + 1)
                wait_count(pe, hT_ready, base + (u - 1))
                for c in range(FC):
                    ins = t_.transpose(hT_ps[u % 2][:, c * P:(c + 1) * P], h[:, u % 2, c * P:(c + 1) * P], ident[:, :])
                ins.then_inc(hT_full, 1)
                if u == PE_UN - 1:
                    for i in range(3):
                        pe.reg_mov(carried[i], expert(base, PE_UN - 2 + i))

            pe.wait_ge(table_ready, 1)
            pe.wait_ge(w_lo_ready, 2 * E)
            pe.wait_ge(bias_in, 32 * NB)
            for k in range(3):
                transpose_rows(0, k)
            first_product(0, 0)
            expert_rounds(pe, step, PE_UN)
            for k in (LAST - 2, LAST - 1):
                second_product((ROUNDS - 1) * UN, k)


_INS = ['L0_attn_x', 'L0_attn_w_qkv', 'L0_attn_w_out', 'L0_attn_b_out', 'L0_ffn_gate_w',
        'L0_ffn_w1', 'L0_ffn_b1', 'L0_ffn_w2', 'L0_ffn_b2']
_OUTS = [((2, 2048, 128), 'float32')]


def kernel(**inputs):
    import numpy as _np
    import concourse.bacc as _bacc
    from concourse import mybir as _mybir
    from concourse.bass_utils import run_bass_kernel_spmd as _run

    nc = _bacc.Bacc("TRN2", target_bir_lowering=False, num_devices=1)
    arrays, args = {}, []
    for name in _INS:
        a = _np.ascontiguousarray(inputs[name])
        arrays[f"in_{name}_dram"] = a
        args.append(nc.dram_tensor(f"in_{name}_dram", a.shape, _mybir.dt.from_np(a.dtype), kind="ExternalInput").ap())
    for i, (shape, dtype) in enumerate(_OUTS):
        dt = _mybir.dt.from_np(_np.dtype(dtype))
        args.append(nc.dram_tensor(f"out_{i}_dram", shape, dt, kind="ExternalOutput").ap())
    preln_attention_moe(nc, *args)
    r = _run(nc, [arrays], core_ids=[0])
    return r.results[0]["out_0_dram"]
```
